# Optimizing a Trainium2 kernel written in Bass

```python
import numpy as np
import jax
import jax.numpy as jnp

def _softmax(x, axis=-1):
    return jax.nn.softmax(x, axis=axis)

def _gelu(x):
    return jax.nn.gelu(x, approximate=True)

def _silu(x):
    return jax.nn.silu(x)

def _sigmoid(x):
    return jax.nn.sigmoid(x)

def _layernorm(x, axis=-1, eps=1e-05):
    m = jnp.mean(x, axis=axis, keepdims=True)
    v = jnp.var(x, axis=axis, keepdims=True)
    return (x - m) / jnp.sqrt(v + eps)

def _scatter_add(tgt, idx, src, axis=0):
    return tgt.at[idx].add(src)

def _segment_sum(src, seg, n):
    return jax.ops.segment_sum(src, seg, n)
kernel_name = 'mk_cond_resid_d2_seqx_r2_de2641'

def setup_inputs(seed: int=0):
    np.random.seed(seed)
    _w = jnp.asarray

    def _rec_inputs():
        import jax
        import jax.numpy as jnp
        _rk = jax.random.key(seed)
        x = -0.0002928 + 1 * jax.random.normal(jax.random.fold_in(_rk, 1), (32, 128, 512), jnp.float32)
        _lenS = 128 - jax.random.randint(jax.random.fold_in(_rk, 7), (32,), 0, max(1, 128 // 4) + 1, jnp.int32)
        _lenS2 = 128 - jax.random.randint(jax.random.fold_in(_rk, 8), (32,), 0, max(1, 128 // 4) + 1, jnp.int32)
        fside_16xSxS_0 = -5.72187e-05 + 0.999849 * jax.random.normal(jax.random.fold_in(_rk, 11), (16, 128, 128), jnp.float32)
        cond_64 = -0.0265395 + 0.99382 * jax.random.normal(jax.random.fold_in(_rk, 13), (32, 64), jnp.float32)
        _validS = jnp.arange(128)[None, :] < _lenS[:, None]
        _validS2 = jnp.arange(128)[None, :] < _lenS2[:, None]
        _causal = jnp.tril(jnp.ones((128, 128), dtype=bool))
        mask_BxS_bk0 = jnp.logical_not(jnp.broadcast_to(_validS[:, :], (32, 128)))
        mask_BxS_bf1 = jnp.ones((32, 128), dtype=bool)
        return (x, fside_16xSxS_0, cond_64, mask_BxS_bk0, mask_BxS_bf1)
    x, fside_16xSxS_0, cond_64, mask_BxS_bk0, mask_BxS_bf1 = _rec_inputs()

    def _L0_cond_setup():
        import jax, jax.numpy as jnp
        import numpy as np
        B, N, DIM, H, DH = (2, 1024, 512, 16, 64)
        INNER = H * DH
        EPS = 1e-05

        def layernorm(x, g):
            mean = jnp.mean(x, axis=-1, keepdims=True)
            var = jnp.var(x, axis=-1, keepdims=True)
            return (x - mean) * jax.lax.rsqrt(var + EPS) * g
        key = jax.random.key(seed)
        ks = jax.random.split(key, 10)
        x = jax.random.normal(ks[0], (B, N, DIM), dtype=jnp.float32)
        attn_bias = jax.random.normal(ks[1], (H, N, N), dtype=jnp.float32)
        mask = jax.random.randint(ks[2], (B, N), 0, 2).astype(bool)
        g_in = jnp.ones((DIM,), dtype=jnp.float32)
        null_attn_bias = jax.random.normal(ks[3], (H,), dtype=jnp.float32)
        null_kv = jax.random.normal(ks[4], (2, DH), dtype=jnp.float32)
        Wq = jax.random.normal(ks[5], (DIM, INNER), dtype=jnp.float32) * 0.02
        Wkv = jax.random.normal(ks[6], (DIM, 2 * DH), dtype=jnp.float32) * 0.02
        Wo = jax.random.normal(ks[7], (INNER, DIM), dtype=jnp.float32) * 0.02
        g_out = jnp.ones((DIM,), dtype=jnp.float32)
        return {'x': x, 'attn_bias': attn_bias, 'mask': mask, 'g_in': g_in, 'null_attn_bias': null_attn_bias, 'null_kv': null_kv, 'Wq': Wq, 'Wkv': Wkv, 'Wo': Wo, 'g_out': g_out}
    _L0_cond_all = _L0_cond_setup()
    _L0_cond_in = {k: v for k, v in _L0_cond_all.items() if k in ('g_in', 'null_attn_bias', 'Wq', 'Wkv', 'Wo', 'g_out')}
    del _L0_cond_all

    def _L1_cond_setup():
        import jax, jax.numpy as jnp
        import numpy as np
        DIM = 512
        HEADS = 16
        DIM_HEAD = 64
        SCALE = 8.0

        def ln(x, g, eps=1e-05):
            mean = x.mean(axis=-1, keepdims=True)
            var = ((x - mean) ** 2).mean(axis=-1, keepdims=True)
            return (x - mean) * jax.lax.rsqrt(var + eps) * g

        def l2norm(t):
            n = jnp.maximum(jnp.linalg.norm(t, axis=-1, keepdims=True), 1e-12)
            return t / n

        def rel_pos_bias(n, w0, b0, g0, w1, b1, g1, w2, b2, dtype):
            pos = jnp.arange(-n + 1, n, dtype=dtype)[:, None]
            h = jax.nn.silu(ln(pos @ w0 + b0, g0))
            h = jax.nn.silu(ln(h @ w1 + b1, g1))
            h = h @ w2 + b2
            i = jnp.arange(n)
            idx = i[:, None] - i[None, :] + n - 1
            bias = h[idx]
            return jnp.transpose(bias, (2, 0, 1))
        key = jax.random.key(seed)
        ks = jax.random.split(key, 16)
        b, n = (2, 1024)
        inner = HEADS * DIM_HEAD
        s = 0.02
        return {'x': jax.random.normal(ks[0], (b, n, DIM), jnp.float32), 'mask': jnp.ones((b, n), dtype=bool), 'g_norm': jnp.ones((DIM,), jnp.float32), 'Wq': jax.random.normal(ks[1], (DIM, inner), jnp.float32) * s, 'Wkv': jax.random.normal(ks[2], (DIM, 2 * DIM_HEAD), jnp.float32) * s, 'q_scale': jnp.ones((DIM_HEAD,), jnp.float32), 'k_scale': jnp.ones((DIM_HEAD,), jnp.float32), 'null_kv': jax.random.normal(ks[3], (2, DIM_HEAD), jnp.float32), 'null_attn_bias': jax.random.normal(ks[4], (HEADS,), jnp.float32), 'w0': jax.random.normal(ks[5], (1, DIM), jnp.float32) * s, 'b0': jnp.zeros((DIM,), jnp.float32), 'g0': jnp.ones((DIM,), jnp.float32), 'w1': jax.random.normal(ks[6], (DIM, DIM), jnp.float32) * s, 'b1': jnp.zeros((DIM,), jnp.float32), 'g1': jnp.ones((DIM,), jnp.float32), 'w2': jax.random.normal(ks[7], (DIM, HEADS), jnp.float32) * s, 'b2': jnp.zeros((HEADS,), jnp.float32), 'Wout': jax.random.normal(ks[8], (inner, DIM), jnp.float32) * s, 'g_out': jnp.ones((DIM,), jnp.float32)}
    _L1_cond_all = _L1_cond_setup()
    _L1_cond_in = {k: v for k, v in _L1_cond_all.items() if k in ('g_norm', 'Wq', 'Wkv', 'q_scale', 'k_scale', 'null_attn_bias', 'w0', 'b0', 'g0', 'w1', 'b1', 'g1', 'w2', 'b2', 'Wout', 'g_out')}
    del _L1_cond_all
    return {'x': x, 'fside_16xSxS_0': fside_16xSxS_0, 'cond_64': cond_64, 'mask_BxS_bk0': mask_BxS_bk0, 'mask_BxS_bf1': mask_BxS_bf1, 'L0_cond_g_in': _L0_cond_in['g_in'], 'L0_cond_null_attn_bias': _L0_cond_in['null_attn_bias'], 'L0_cond_Wq': _L0_cond_in['Wq'], 'L0_cond_Wkv': _L0_cond_in['Wkv'], 'L0_cond_Wo': _L0_cond_in['Wo'], 'L0_cond_g_out': _L0_cond_in['g_out'], 'L1_cond_g_norm': _L1_cond_in['g_norm'], 'L1_cond_Wq': _L1_cond_in['Wq'], 'L1_cond_Wkv': _L1_cond_in['Wkv'], 'L1_cond_q_scale': _L1_cond_in['q_scale'], 'L1_cond_k_scale': _L1_cond_in['k_scale'], 'L1_cond_null_attn_bias': _L1_cond_in['null_attn_bias'], 'L1_cond_w0': _L1_cond_in['w0'], 'L1_cond_b0': _L1_cond_in['b0'], 'L1_cond_g0': _L1_cond_in['g0'], 'L1_cond_w1': _L1_cond_in['w1'], 'L1_cond_b1': _L1_cond_in['b1'], 'L1_cond_g1': _L1_cond_in['g1'], 'L1_cond_w2': _L1_cond_in['w2'], 'L1_cond_b2': _L1_cond_in['b2'], 'L1_cond_Wout': _L1_cond_in['Wout'], 'L1_cond_g_out': _L1_cond_in['g_out']}

def reference(x, fside_16xSxS_0, cond_64, mask_BxS_bk0, mask_BxS_bf1, L0_cond_g_in, L0_cond_null_attn_bias, L0_cond_Wq, L0_cond_Wkv, L0_cond_Wo, L0_cond_g_out, L1_cond_g_norm, L1_cond_Wq, L1_cond_Wkv, L1_cond_q_scale, L1_cond_k_scale, L1_cond_null_attn_bias, L1_cond_w0, L1_cond_b0, L1_cond_g0, L1_cond_w1, L1_cond_b1, L1_cond_g1, L1_cond_w2, L1_cond_b2, L1_cond_Wout, L1_cond_g_out):
    import jax
    import jax.numpy as jnp

    def _L0_cond_ref(x, attn_bias, mask, g_in, null_attn_bias, null_kv, Wq, Wkv, Wo, g_out):
        import jax, jax.numpy as jnp
        import numpy as np
        B, N, DIM, H, DH = (2, 1024, 512, 16, 64)
        INNER = H * DH
        EPS = 1e-05

        def layernorm(x, g):
            mean = jnp.mean(x, axis=-1, keepdims=True)
            var = jnp.var(x, axis=-1, keepdims=True)
            return (x - mean) * jax.lax.rsqrt(var + EPS) * g
        b, n, _ = x.shape
        scale = DH ** (-0.5)
        xn = layernorm(x, g_in)
        q = (xn @ Wq).reshape(b, n, H, DH).transpose(0, 2, 1, 3) * scale
        kv = xn @ Wkv
        k, v = (kv[..., :DH], kv[..., DH:])
        nk = jnp.broadcast_to(null_kv[0], (b, 1, DH))
        nv = jnp.broadcast_to(null_kv[1], (b, 1, DH))
        k = jnp.concatenate([nk, k], axis=1)
        v = jnp.concatenate([nv, v], axis=1)
        sim = jnp.einsum('bhid,bjd->bhij', q, k)
        null_col = jnp.broadcast_to(null_attn_bias[:, None, None], (H, n, 1))
        bias = jnp.concatenate([null_col, attn_bias], axis=-1)
        sim = sim + bias
        neg = -jnp.finfo(sim.dtype).max
        j = n + 1
        causal_mask = jnp.triu(jnp.ones((n, j), dtype=bool), k=j - n + 1)
        sim = jnp.where(causal_mask, neg, sim)
        mask_p = jnp.pad(mask, ((0, 0), (1, 0)), constant_values=True)
        sim = jnp.where(mask_p[:, None, None, :], sim, neg)
        attn = jax.nn.softmax(sim, axis=-1)
        out = jnp.einsum('bhij,bjd->bhid', attn, v)
        out = out.transpose(0, 2, 1, 3).reshape(b, n, INNER)
        out = out @ Wo
        return layernorm(out, g_out)

    def _L1_cond_ref(x, mask, g_norm, Wq, Wkv, q_scale, k_scale, null_kv, null_attn_bias, w0, b0, g0, w1, b1, g1, w2, b2, Wout, g_out):
        import jax, jax.numpy as jnp
        import numpy as np
        DIM = 512
        HEADS = 16
        DIM_HEAD = 64
        SCALE = 8.0

        def ln(x, g, eps=1e-05):
            mean = x.mean(axis=-1, keepdims=True)
            var = ((x - mean) ** 2).mean(axis=-1, keepdims=True)
            return (x - mean) * jax.lax.rsqrt(var + eps) * g

        def l2norm(t):
            n = jnp.maximum(jnp.linalg.norm(t, axis=-1, keepdims=True), 1e-12)
            return t / n

        def rel_pos_bias(n, w0, b0, g0, w1, b1, g1, w2, b2, dtype):
            pos = jnp.arange(-n + 1, n, dtype=dtype)[:, None]
            h = jax.nn.silu(ln(pos @ w0 + b0, g0))
            h = jax.nn.silu(ln(h @ w1 + b1, g1))
            h = h @ w2 + b2
            i = jnp.arange(n)
            idx = i[:, None] - i[None, :] + n - 1
            bias = h[idx]
            return jnp.transpose(bias, (2, 0, 1))
        b, n, _ = x.shape
        xn = ln(x, g_norm)
        q = (xn @ Wq).reshape(b, n, HEADS, DIM_HEAD).transpose(0, 2, 1, 3)
        kv = xn @ Wkv
        k, v = (kv[..., :DIM_HEAD], kv[..., DIM_HEAD:])
        nk = jnp.broadcast_to(null_kv[0], (b, 1, DIM_HEAD))
        nv = jnp.broadcast_to(null_kv[1], (b, 1, DIM_HEAD))
        k = jnp.concatenate([nk, k], axis=1)
        v = jnp.concatenate([nv, v], axis=1)
        q = l2norm(q) * q_scale
        k = l2norm(k) * k_scale
        sim = jnp.einsum('bhid,bjd->bhij', q, k) * SCALE
        bias = rel_pos_bias(n, w0, b0, g0, w1, b1, g1, w2, b2, q.dtype)
        null_bias = jnp.broadcast_to(null_attn_bias[:, None, None], (HEADS, n, 1))
        attn_bias = jnp.concatenate([null_bias, bias], axis=-1)
        sim = sim + attn_bias
        neg = -jnp.finfo(sim.dtype).max
        causal = jnp.triu(jnp.ones((n, n + 1), dtype=bool), k=2)
        sim = jnp.where(causal, neg, sim)
        m = jnp.pad(mask, ((0, 0), (1, 0)), constant_values=True)[:, None, None, :]
        sim = jnp.where(m, sim, neg)
        attn = jax.nn.softmax(sim, axis=-1)
        out = jnp.einsum('bhij,bjd->bhid', attn, v)
        out = out.transpose(0, 2, 1, 3).reshape(b, n, HEADS * DIM_HEAD)
        return ln(out @ Wout, g_out)
    x = x + _L0_cond_ref(x, fside_16xSxS_0, mask_BxS_bk0, L0_cond_g_in, L0_cond_null_attn_bias, cond_64, L0_cond_Wq, L0_cond_Wkv, L0_cond_Wo, L0_cond_g_out)
    x = x + _L1_cond_ref(x, mask_BxS_bf1, L1_cond_g_norm, L1_cond_Wq, L1_cond_Wkv, L1_cond_q_scale, L1_cond_k_scale, cond_64, L1_cond_null_attn_bias, L1_cond_w0, L1_cond_b0, L1_cond_g0, L1_cond_w1, L1_cond_b1, L1_cond_g1, L1_cond_w2, L1_cond_b2, L1_cond_Wout, L1_cond_g_out)
    return x

_drawn_inputs = setup_inputs


def setup_inputs(seed=0):
    import zlib

    import numpy as np

    out = dict(_drawn_inputs(seed))
    spreads = {'L0_cond_g_in': (1.0, 0.536),
     'L0_cond_g_out': (1.0, 0.2),
     'L1_cond_g_norm': (1.0, 0.2),
     'L1_cond_q_scale': (1.0, 0.572),
     'L1_cond_k_scale': (1.0, 0.2),
     'L1_cond_b0': (0.0, 0.303),
     'L1_cond_g0': (1.0, 0.6),
     'L1_cond_b1': (0.0, 0.8),
     'L1_cond_g1': (1.0, 0.6),
     'L1_cond_b2': (0.0, 0.8),
     'L1_cond_g_out': (1.0, 0.2)}
    factors = {'L1_cond_w0': 2.866}
    for name, (base, spread) in spreads.items():
        noise = np.random.default_rng([zlib.crc32(name.encode()), seed]).standard_normal(out[name].shape)
        drawn = base * np.exp(spread * noise) if base else spread * noise
        out[name] = jnp.asarray(drawn.astype(out[name].dtype))
    for name, factor in factors.items():
        out[name] = (out[name] * factor).astype(out[name].dtype)
    return out
```

```python
from contextlib import ExitStack

import concourse.bass as bass
from concourse import mybir

ALU = mybir.AluOpType
ACT = mybir.ActivationFunctionType
AX = mybir.AxisListType
F32 = mybir.dt.float32
F32R = mybir.dt.float32r
I32 = mybir.dt.int32
U8 = mybir.dt.uint8

P = 128
B = 32
D = 512
H = 16
DH = 64
INNER = H * DH
LAYERS = 2
N = LAYERS * B
KC = D // P
OC = INNER // P
QKV = INNER + 2 * DH
W = QKV + H
G = 4
HG = H // G
PARTS = [(0, 6), (6, 6), (12, 4)]
EPS = 1e-5
TINY = 1e-24
BIG = 1e38
LOWEST = -3.4e38
FIRST, LAST = 3, B - 4


def part_columns(p):
    first, count = PARTS[p]
    return first * DH, (W if p == len(PARTS) - 1 else (first + count) * DH)


def count(m, d=0):
    layer, b = m
    return b + (layer * B + 1 + d)


def wait(e, sem, m, d=0, by=1):
    value = count(m, d) * by
    if not (isinstance(value, int) and value <= 0):
        e.wait_ge(sem, value)


def wait_in_layer1(e, sem, m, d=0):
    value = m[1] + (1 + d)
    if not (isinstance(value, int) and value <= 0):
        e.wait_ge(sem, value)


def opens_layer(m):
    return isinstance(m[1], int) and m[1] == 0


def stream(e, step, between=None):
    def straight(first, last):
        for n in range(first, last):
            if between:
                between(n)
            step(lambda d, n=n: ((n + d) // B, (n + d) % B) if 0 <= n + d < N else None)

    straight(-3, FIRST)
    for layer in range(LAYERS):
        with e.Fori(FIRST, LAST + 1) as i:
            step(lambda d: (layer, i + d))
        straight(layer * B + LAST + 1, (layer + 1) * B + FIRST if layer + 1 < LAYERS else N + 2)


def build(nc, x, bias0, cond, mask0, mask1, g_in, null_bias, wq, wkv, wo, g_out, q_scale, k_scale,
          w0, b0, g0, w1, b1, g1, w2, b2, out):
    x_mid = nc.dram_tensor("x_mid", (B, P, D), F32, kind="Internal").ap()
    table = nc.dram_tensor("bias_table", (H, P, 2 * P), F32, kind="Internal").ap()
    x_of = [x, x_mid]
    out_of = [x_mid, out]

    with ExitStack() as ctx:
        def sb(name, shape, dt=F32):
            return ctx.enter_context(nc.sbuf_tensor(name, shape, dt))

        def psum(name):
            return ctx.enter_context(nc.psum_tensor(name, [P, 512], F32))

        def sem(name):
            return ctx.enter_context(nc.semaphore(name))

        def sems(name, n):
            return [sem(f"{name}{i}") for i in range(n)]

        wq_h = sb("wq_h", [P, KC, W], F32R)
        wq_l = sb("wq_l", [P, KC, W], F32R)
        wo_h = sb("wo_h", [P, OC, D], F32R)
        wo_l = sb("wo_l", [P, OC, D], F32R)
        wq_raw = sb("wq_raw", [P, KC, QKV])
        wo_raw = sb("wo_raw", [P, OC, D])
        w_null = sb("w_null", [P, KC, H])
        bias = sb("bias", [P, LAYERS, H, P])
        mask = sb("mask", [P, LAYERS, B, P], U8)
        g_in_sb = sb("g_in_sb", [P, LAYERS, KC])
        g_out_sb = sb("g_out_sb", [P, LAYERS, D])
        null_bias_sb = sb("null_bias_sb", [P, LAYERS, H])
        null_k = sb("null_k", [P, DH])
        null_kn = sb("null_kn", [P, LAYERS, DH])
        null_v = sb("null_v", [P, DH])
        null_v_col = sb("null_v_col", [P, 1])
        qs = sb("qs", [P, DH])
        k_mul = sb("k_mul", [P, DH])
        nk_sq = sb("nk_sq", [P, DH])
        nk_ss = sb("nk_ss", [P, 2])
        ident = sb("ident", [P, P])
        minus_half = sb("minus_half", [P, 8])
        x_in = sb("x_in", [P, D])
        x_res = sb("x_res", [P, D])
        xn = sb("xn", [P, D])
        xt_h = sb("xt_h", [P, KC, P], F32R)
        xt_l = sb("xt_l", [P, KC, P], F32R)
        q_nat = sb("q_nat", [P, INNER])
        squares = sb("squares", [P, 6 * DH])
        k_nat = sb("k_nat", [P, 2, DH])
        v_raw = sb("v_raw", [P, DH])
        ln_st = sb("ln_st", [P, 6])
        ln_mv = sb("ln_mv", [P, 2])
        ln_ve = sb("ln_ve", [P, 1])
        ln_rstd = sb("ln_rstd", [P, 1])
        y_st = sb("y_st", [P, 6])
        y_mv = sb("y_mv", [P, 2])
        y_ve = sb("y_ve", [P, 1])
        y_rstd = sb("y_rstd", [P, 1])
        ss = sb("ss", [P, H + 1])
        ssc = sb("ssc", [P, H + 1])
        rnorm = sb("rnorm", [P, H + 1])
        null_s = sb("null_s", [P, H])
        nns_next = sb("nns_next", [P, H])
        nns = sb("nns", [P, H])
        qt_h = sb("qt_h", [P, OC, P], F32R)
        qt_l = sb("qt_l", [P, OC, P], F32R)
        kt_h = sb("kt_h", [P, 2, P], F32R)
        kt_l = sb("kt_l", [P, 2, P], F32R)
        v_h = sb("v_h", [P, 2 * P], F32R)
        v_l = sb("v_l", [P, 2 * P], F32R)
        mask_row = sb("mask_row", [P, P])
        bias_g = sb("bias_g", [P, 2, HG, P])
        s_sb = sb("s_sb", [P, 2, HG, P])
        mx = sb("mx", [P, H])
        neg_m = sb("neg_m", [P, H])
        d_null = sb("d_null", [P, H])
        p_null = sb("p_null", [P, H])
        esum = sb("esum", [P, H])
        den = sb("den", [P, H])
        rden = sb("rden", [P, H])
        p_raw = sb("p_raw", [P, 2, HG, P])
        p_sb = sb("p_sb", [P, 2, HG, P])
        pt_h = sb("pt_h", [P, 2, HG, P], F32R)
        pt_l = sb("pt_l", [P, 2, HG, P], F32R)
        ot_h = sb("ot_h", [P, OC, P], F32R)
        ot_l = sb("ot_l", [P, OC, P], F32R)
        y_out = sb("y_out", [P, 2, D])
        y_t, x_out = y_out[:, 0, :], y_out[:, 1, :]
        w1_sb = sb("w1_sb", [P, KC, D])
        w2_sb = sb("w2_sb", [P, KC, H])
        b2_col = sb("b2_col", [H, 1])
        pos_i = sb("pos_i", [P, 1], I32)
        pos = sb("pos", [P, 1])
        table_sb = squares[0:H, 0:2 * P]
        flat = lambda t: t[:, :, :, :].rearrange("p a h j -> p a (h j)")
        w0_b, b0_b = flat(p_raw)[:, 0, :], flat(p_raw)[:, 1, :]
        g_b, b1_b = [flat(p_sb)[:, 0, :], flat(p_sb)[:, 1, :]], q_nat[:, 0:D]
        net = flat(s_sb)[:, 0, :]
        net_t = flat(s_sb)[:, 1, :].rearrange("p (c t) -> p c t", c=KC)
        net_e = q_nat[:, D:2 * D]

        bank_s = [psum("bank_s0"), psum("bank_s1")]
        bank_p = psum("bank_p")
        bank_q = [psum("bank_q0"), psum("bank_q1")]
        bank_o = psum("bank_o")
        bank_t = psum("bank_t")
        bank_y = psum("bank_y")

        wq_loaded = sem("wq_loaded")
        wo_loaded = sem("wo_loaded")
        small_loaded = sem("small_loaded")
        rows_loaded = sem("rows_loaded")
        bias0_loaded = sem("bias0_loaded")
        net_loaded = sem("net_loaded")
        table_stored = sem("table_stored")
        bias1_loaded = sem("bias1_loaded")
        consts_ready = sem("consts_ready")
        zeros_ready = sem("zeros_ready")
        causal_ready = sem("causal_ready")
        nk_step = sem("nk_step")
        null_prod = sem("null_prod")
        null_ready = sem("null_ready")
        wq_h_ready = sem("wq_h_ready")
        wn_h_ready = sem("wn_h_ready")
        wq_ready = sem("wq_ready")
        wo_h_ready = sem("wo_h_ready")
        wo_ready = sem("wo_ready")
        net_step = sem("net_step")
        x_loaded = sem("x_loaded")
        res_loaded = sem("res_loaded")
        x_stored = sem("x_stored")
        ln_st_done = sem("ln_st_done")
        ln_mv_done = sem("ln_mv_done")
        ln_ve_done = sem("ln_ve_done")
        ln_rstd_done = sem("ln_rstd_done")
        xn_ready = sem("xn_ready")
        xt_psum = sem("xt_psum")
        xt_h_ready = sem("xt_h_ready")
        xt_ready = sem("xt_ready")
        q_psum = sems("q_psum", 3)
        q_copied = sem("q_copied")
        squares_ready = sems("squares_ready", 3)
        q_sum = sems("q_sum", 3)
        q_clamp = sems("q_clamp", 3)
        q_norm = sems("q_norm", 3)
        q_done = sems("q_done", 3)
        null_s_done = sem("null_s_done")
        nns_next_ready = sem("nns_next_ready")
        nns_ready = sem("nns_ready")
        qt_psum = sems("qt_psum", 2)
        qt_h_ready = sems("qt_h_ready", 2)
        qt_ready = sems("qt_ready", 2)
        kt_psum = sem("kt_psum")
        kt_h_ready = sem("kt_h_ready")
        kt_ready = sem("kt_ready")
        v_h_ready = sem("v_h_ready")
        v_ready = sem("v_ready")
        mask_ready = sem("mask_ready")
        bias_ready = sems("bias_ready", G)
        s_psum = sems("s_psum", G)
        s_ready = sems("s_ready", G)
        neg_m_ready = sems("neg_m_ready", G)
        d_null_ready = sems("d_null_ready", G)
        exp_ready = sems("exp_ready", G)
        den_ready = sems("den_ready", G)
        rden_ready = sems("rden_ready", G)
        p_ready = sems("p_ready", G)
        pt_psum = sems("pt_psum", G)
        pt_h_ready = sems("pt_h_ready", G)
        pt_ready = sems("pt_ready", G)
        pv_psum = sems("pv_psum", G)
        ot_h_ready = sems("ot_h_ready", 2)
        ot_ready = sems("ot_ready", 2)
        wo_half = sems("wo_half", 2)
        y_st_done = sem("y_st_done")
        y_mv_done = sem("y_mv_done")
        y_ve_done = sem("y_ve_done")
        y_rstd_done = sem("y_rstd_done")
        y_out_of_psum = sem("y_out_of_psum")
        x_out_ready = sem("x_out_ready")

        WQ_LOADS, WO_LOADS = 2, 1
        SMALL_LOADS = 6 + 2 * LAYERS
        ROW_LOADS = 2 * LAYERS
        NET_LOADS = 8
        (POS, PRE1, ST1, MV1, VE1, RSTD1, CEN1, GAIN1, EXP1, PLUS1, REC1, SILU1, TP1, TCOPY1,
         MM1, PRE2, ST2, MV2, VE2, RSTD2, CEN2, GAIN2, EXP2, PLUS2, REC2, SILU2, TP2, TCOPY2,
         MM2, TABLE) = range(1, 31)

        block = ctx.enter_context(nc.Block())

        @block.sync
        def _(e):
            def load_wq(layer):
                e.dma_start(wq_raw[:, :, 0:INNER], wq[layer].rearrange("(c p) n -> p c n", p=P)).then_inc(wq_loaded, 16)
                e.dma_start(wq_raw[:, :, INNER:QKV], wkv[layer].rearrange("(c p) n -> p c n", p=P)).then_inc(wq_loaded, 16)

            def load_wo(layer):
                e.dma_start(wo_raw[:, :, :], wo[layer].rearrange("(c p) n -> p c n", p=P)).then_inc(wo_loaded, 16)

            def row(v):
                return v.rearrange("(a n) -> a n", a=1)

            def small(dst, src, **how):
                e.dma_start(dst, src, **how).then_inc(small_loaded, 16)

            small(null_k[:, :], cond[0:1, :].broadcast_to([P, DH]))
            small(qs[:, :], row(q_scale).broadcast_to([P, DH]))
            small(k_mul[:, :], row(k_scale).broadcast_to([P, DH]))
            small(null_v[:, :], cond[1:2, :].broadcast_to([P, DH]))
            for half in range(2):
                small(null_v_col[half * DH:(half + 1) * DH, :], cond[1:2, :].rearrange("a d -> d a"))
            for layer in range(LAYERS):
                small(g_in_sb[:, layer, :], g_in[layer].rearrange("(c p) -> p c", p=P), allow_slow_non_contiguous=True)
                small(null_bias_sb[:, layer, :], row(null_bias[layer]).broadcast_to([P, H]))
            load_wq(0)
            for layer in range(LAYERS):
                e.dma_start(g_out_sb[:, layer, :], row(g_out[layer]).broadcast_to([P, D])).then_inc(rows_loaded, 16)
                m = (mask0, mask1)[layer].rearrange("(a b) s -> a b s", a=1)
                e.dma_start(mask[:, layer, :, :], m.broadcast_to([P, B, P])).then_inc(rows_loaded, 16)
            e.dma_start(bias[:, 0, :, :], bias0.rearrange("h i j -> i h j")).then_inc(bias0_loaded, 16)
            load_wo(0)

            def step(at):
                if (m := at(-2)) is not None:
                    wait(e, x_out_ready, m)
                    e.dma_start(out_of[m[0]][m[1]], x_out).then_inc(x_stored, 16)
                if (m := at(-1)) is not None:
                    wait(e, x_out_ready, m, -1)
                    e.dma_start(x_res[:, :], x_of[m[0]][m[1]]).then_inc(res_loaded, 16)
                if (m := at(3)) is not None:
                    wait(e, xn_ready, m, -1)
                    if m[0] == 1:
                        e.wait_ge(x_stored, (m[1] + 1) * 16)
                    e.dma_start(x_in[:, :], x_of[m[0]][m[1]]).then_inc(x_loaded, 16)

            def between(n):
                if n == -1:
                    e.wait_ge(wq_ready, 1)
                    load_wq(1)
                if n == 0:
                    e.wait_ge(wo_ready, 1)
                    load_wo(1)
                    e.wait_ge(net_step, TABLE)
                    e.dma_start(table, table_sb.unsqueeze(1).broadcast_to([H, P, 2 * P])).then_inc(table_stored, 16)
                if n == 1:
                    e.wait_ge(table_stored, 16)
                    shifted = bass.AP(table.tensor, P - 1, [[2 * P - 1, P], [2 * P * P, H], [1, P]])
                    e.dma_start(bias[:, 1, :, :], shifted)\
                        .then_inc(bias1_loaded, 16)

            stream(e, step, between)
            e.wait_ge(x_stored, 16 * N)

        @block.gpsimd
        def _(e):
            e.memset(ident[:, :], 0.0).then_inc(consts_ready, 1)
            e.memset(minus_half[:, :], -0.5).then_inc(consts_ready, 1)
            e.iota(pos_i[:, :], pattern=[[0, 1]], base=P - 1, channel_multiplier=-1).then_inc(consts_ready, 1)
            e.wait_ge(consts_ready, 3)
            e.affine_select(out=ident[:, :], in_=ident[:, :], compare_op=ALU.not_equal, fill=1.0, base=0,
                            pattern=[[-1, P]], channel_multiplier=1).then_inc(consts_ready, 1)
            e.wait_ge(nk_step, 4)
            e.tensor_tensor(nk_ss[:, 1:2], nk_ss[:, 0:1], minus_half[:, 0:1], ALU.pow).then_inc(nk_step, 1)
            for ve, rstd in ((VE1, RSTD1), (VE2, RSTD2)):
                e.wait_ge(net_step, ve)
                e.tensor_tensor(ln_rstd[:, :], ln_ve[:, :], minus_half[:, 0:1], ALU.pow).then_inc(net_step, 1)
            e.wait_ge(bias0_loaded, 16)
            e.affine_select(out=bias[:, 0, :, :], in_=bias[:, 0, :, :], compare_op=ALU.is_ge, fill=-BIG, base=0,
                            pattern=[[0, H], [-1, P]], channel_multiplier=1).then_inc(causal_ready, 1)

            def masked_bias(m, g):
                if opens_layer(m) and g == 0:
                    if m[0] == 0:
                        e.wait_ge(causal_ready, 1)
                    else:
                        e.wait_ge(bias1_loaded, 16)
                if g == 0:
                    wait(e, mask_ready, m)
                wait(e, s_ready[(g + 2) % G], m, -1 if g < 2 else 0)
                e.tensor_tensor(bias_g[:, g % 2, :, :], bias[:, m[0], HG * g:HG * (g + 1), :],
                                mask_row[:, :].unsqueeze(1).broadcast_to([P, HG, P]), ALU.add)\
                    .then_inc(bias_ready[g], 1)

            def normalise(m, g):
                wait(e, rden_ready[g], m)
                wait(e, pt_psum[(g + 2) % G], m, -1 if g < 2 else 0)
                r = rden[:, HG * g:HG * (g + 1)].unsqueeze(2).broadcast_to([P, HG, P])
                e.tensor_tensor(p_sb[:, g % 2, :, :], p_raw[:, g % 2, :, :], r, ALU.mult).then_inc(p_ready[g], 1)

            def norms(m, p):
                if m[0] == 0:
                    return
                first, n = PARTS[p]
                n += p == 2
                wait_in_layer1(e, q_clamp[p], m)
                e.tensor_tensor(rnorm[:, first:first + n], ssc[:, first:first + n], minus_half[:, 0:n], ALU.pow)\
                    .then_inc(q_norm[p], 1)

            def step(at):
                m, after, prev, later = at(0), at(1), at(-1), at(2)
                if prev is not None:
                    normalise(prev, 3)
                if m is not None:
                    masked_bias(m, 1)
                if later is not None:
                    wait(e, ln_ve_done, later)
                    e.tensor_tensor(ln_rstd[:, :], ln_ve[:, :], minus_half[:, 0:1], ALU.pow).then_inc(ln_rstd_done, 1)
                if m is not None:
                    normalise(m, 0)
                if after is not None:
                    norms(after, 0)
                if m is not None:
                    masked_bias(m, 2)
                    normalise(m, 1)
                if after is not None:
                    norms(after, 1)
                if m is not None:
                    masked_bias(m, 3)
                    normalise(m, 2)
                if after is not None:
                    norms(after, 2)
                    masked_bias(after, 0)
                if prev is not None:
                    wait(e, y_ve_done, prev)
                    e.tensor_tensor(y_rstd[:, :], y_ve[:, :], minus_half[:, 0:1], ALU.pow).then_inc(y_rstd_done, 1)

            stream(e, step)

        @block.scalar
        def _(e):
            def net_load(dst, src):
                e.dma_start(dst, src).then_inc(net_loaded, 16)

            def row(v):
                return v.rearrange("(a n) -> a n", a=1).broadcast_to([P, D])

            net_load(w0_b, w0.broadcast_to([P, D]))
            net_load(b0_b, row(b0))
            net_load(g_b[0], row(g0))
            net_load(g_b[1], row(g1))
            net_load(b1_b, row(b1))
            net_load(w1_sb[:, :, :], w1.rearrange("(c p) n -> p c n", p=P))
            net_load(w2_sb[:, :, :], w2.rearrange("(c p) n -> p c n", p=P))
            net_load(b2_col[:, :], b2.rearrange("(h a) -> h a", a=1))

            def net_silu(gain, exp):
                e.wait_ge(net_step, gain)
                e.activation(net_e, net, ACT.Exp, scale=-1.0).then_inc(net_step, 1)

            def net_copy(tp, copy):
                e.wait_ge(net_step, tp)
                e.activation(net_t, bank_t[:, :].rearrange("p (c t) -> p c t", c=KC), ACT.Copy).then_inc(net_step, 1)

            def project_weights(layer):
                e.wait_ge(wq_loaded, 16 * WQ_LOADS * (layer + 1))
                e.wait_ge(small_loaded, 16 * SMALL_LOADS)
                if layer:
                    e.wait_ge(q_psum[2], B)
                for c in range(KC):
                    e.activation(wq_h[:, c, 0:QKV], wq_raw[:, c, :], ACT.Copy, scale=g_in_sb[:, layer, c:c + 1])\
                        .then_inc(wq_h_ready, 1)
                e.wait_ge(null_ready, KC * (layer + 1))
                for c in range(KC):
                    e.activation(wq_h[:, c, QKV:W], w_null[:, c, :], ACT.Copy, scale=g_in_sb[:, layer, c:c + 1])\
                        .then_inc(wn_h_ready, 1)

            def output_weights(layer):
                e.wait_ge(wo_loaded, 16 * WO_LOADS * (layer + 1))
                if layer:
                    e.wait_ge(wo_half[1], B)
                for c in range(OC):
                    e.activation(wo_h[:, c, :], wo_raw[:, c, :], ACT.Copy).then_inc(wo_h_ready, 1)

            def split_xt(m):
                wait(e, xt_psum, m)
                wait(e, q_psum[2], m, -1)
                e.activation(xt_h[:, :, :], bank_t[:, :].rearrange("p (c t) -> p c t", c=KC), ACT.Copy)\
                    .then_inc(xt_h_ready, 1)

            def q_out(m, p):
                first, n = PARTS[p]
                wait(e, q_psum[p], m)
                if m[0] == 0:
                    wait(e, qt_psum[1], m, -1)
                    e.activation(q_nat[:, first * DH:(first + n) * DH], bank_q[p % 2][:, 0:n * DH], ACT.Copy)\
                        .then_inc(q_done[p] if p < 2 else q_copied, 1)
                else:
                    n += p == 2
                    wait_in_layer1(e, q_sum[(p + 2) % 3], m, 0 if p else -1)
                    e.activation(squares[:, 0:n * DH], bank_q[p % 2][:, 0:n * DH], ACT.Square)\
                        .then_inc(squares_ready[p], 1)

            def split_qt(m, half):
                wait(e, qt_psum[half], m)
                wait(e, s_psum[2 * half + 1], m, -1)
                e.activation(qt_h[:, 4 * half:4 * half + 4, :], bank_t[:, :].rearrange("p (c t) -> p c t", c=4),
                             ACT.Copy).then_inc(qt_h_ready[half], 1)

            def split_kt(m):
                wait(e, kt_psum, m)
                wait(e, s_psum[3], m, -1)
                for half in range(2):
                    r = slice(half * DH, (half + 1) * DH)
                    last = e.activation(kt_h[r, half, :], bank_t[r, 0:P], ACT.Copy)
                last.then_inc(kt_h_ready, 1)

            def split_v(m):
                wait(e, q_done[2], m)
                wait(e, pv_psum[3], m, -1)
                v2 = v_h[:, 0:2 * P].rearrange("p (a b d) -> p a b d", a=2, b=2)
                for half in range(2):
                    last = e.activation(v2[:, half, half, :], v_raw[:, :], ACT.Copy)
                last.then_inc(v_h_ready, 1)

            def exps(m, g):
                wait(e, d_null_ready[g], m)
                wait(e, p_ready[(g + 2) % G], m, -1 if g < 2 else 0)
                for j in range(HG):
                    h = HG * g + j
                    e.activation(p_raw[:, g % 2, j, :], s_sb[:, g % 2, j, :], ACT.Exp, bias=neg_m[:, h:h + 1],
                                 accum_out=esum[:, h:h + 1])
                e.activation(p_null[:, HG * g:HG * (g + 1)], d_null[:, HG * g:HG * (g + 1)], ACT.Exp)\
                    .then_inc(exp_ready[g], 1)

            def split_pt(m, g):
                wait(e, pt_psum[g], m)
                wait(e, pv_psum[(g + 2) % G], m, -1 if g < 2 else 0)
                e.activation(pt_h[:, g % 2, :, :], bank_p[:, :].rearrange("p (h i) -> p h i", h=HG), ACT.Copy)\
                    .then_inc(pt_h_ready[g], 1)

            def split_ot(m, half):
                wait(e, pv_psum[2 * half + 1], m)
                wait(e, wo_half[half], m, -1)
                e.activation(ot_h[:, 4 * half:4 * half + 4, :], bank_o[:, :].rearrange("p (c t) -> p c t", c=4),
                             ACT.Identity, bias=null_v_col[:, :]).then_inc(ot_h_ready[half], 1)

            def step(at):
                m, after, prev, later = at(0), at(1), at(-1), at(2)
                if prev is not None:
                    split_ot(prev, 0)
                if m is not None:
                    exps(m, 0)
                if prev is not None:
                    split_pt(prev, 3)
                if after is not None:
                    q_out(after, 0)
                if m is not None:
                    exps(m, 1)
                    split_pt(m, 0)
                if after is not None:
                    q_out(after, 1)
                if prev is not None:
                    split_ot(prev, 1)
                if m is not None:
                    split_v(m)
                    exps(m, 2)
                if after is not None:
                    q_out(after, 2)
                if m is not None:
                    split_pt(m, 1)
                if after is not None:
                    split_qt(after, 0)
                if m is not None:
                    exps(m, 3)
                if after is not None:
                    split_qt(after, 1)
                    split_kt(after)
                if m is not None:
                    split_pt(m, 2)
                if later is not None:
                    split_xt(later)

            def between(n):
                if n == B - 1:
                    project_weights(1)
                if n == B + 1:
                    output_weights(1)

            net_silu(GAIN1, EXP1)
            net_copy(TP1, TCOPY1)
            net_silu(GAIN2, EXP2)
            net_copy(TP2, TCOPY2)
            project_weights(0)
            output_weights(0)
            stream(e, step, between)

        @block.vector
        def _(e):
            for t in (kt_h, kt_l):
                e.memset(t[:, :, :].bitcast(F32), 0.0)
            e.memset(v_h[:, :].bitcast(F32), 0.0)
            e.memset(v_l[:, :].bitcast(F32), 0.0).then_inc(zeros_ready, 1)
            e.wait_ge(zeros_ready, 1)

            e.wait_ge(small_loaded, 16 * SMALL_LOADS)
            e.tensor_scalar(null_kn[:, 0, :], null_k[:, :], DH ** -0.5, None, ALU.mult)
            e.tensor_tensor(nk_sq[:, :], null_k[:, :], null_k[:, :], ALU.mult).then_inc(nk_step, 1)
            e.scalar_tensor_tensor(out=k_mul[:, :], in0=k_mul[:, :], scalar=8.0, in1=qs[:, :], op0=ALU.mult,
                                   op1=ALU.mult).then_inc(nk_step, 1)
            e.wait_ge(nk_step, 2)
            e.reduce_sum(nk_ss[:, 1:2], nk_sq[:, :], AX.X).then_inc(nk_step, 1)
            e.wait_ge(nk_step, 3)
            e.tensor_scalar(nk_ss[:, 0:1], nk_ss[:, 1:2], TINY, None, ALU.max).then_inc(nk_step, 1)
            e.wait_ge(consts_ready, 4)
            e.wait_ge(nk_step, 5)
            e.scalar_tensor_tensor(out=null_kn[:, 1, :], in0=null_k[:, :], scalar=nk_ss[:, 1:2], in1=k_mul[:, :],
                                   op0=ALU.mult, op1=ALU.mult).then_inc(nk_step, 1)

            def null_columns(layer, scratch):
                e.wait_ge(nk_step, 6)
                e.wait_ge(wq_loaded, 16 * WQ_LOADS * (layer + 1))
                s = scratch.rearrange("p (h d) -> p h d", h=H)
                for c in range(KC):
                    k = KC * layer + c
                    if k:
                        e.wait_ge(null_ready, k)
                    e.tensor_tensor(s, wq_raw[:, c, 0:INNER].rearrange("p (h d) -> p h d", h=H),
                                    null_kn[:, layer, :].unsqueeze(1).broadcast_to([P, H, DH]), ALU.mult)\
                        .then_inc(null_prod, 1)
                    e.wait_ge(null_prod, k + 1)
                    if layer:
                        e.wait_ge(wn_h_ready, KC)
                    e.reduce_sum(w_null[:, c, :], s, AX.X).then_inc(null_ready, 1)

            def project_weights(layer):
                if layer:
                    e.wait_ge(q_psum[2], B)
                for c in range(KC):
                    e.wait_ge(wq_h_ready, KC * layer + c + 1)
                    e.scalar_tensor_tensor(out=wq_l[:, c, 0:QKV], in0=wq_raw[:, c, :],
                                           scalar=g_in_sb[:, layer, c:c + 1], in1=wq_h[:, c, 0:QKV].bitcast(F32),
                                           op0=ALU.mult, op1=ALU.subtract)
                for c in range(KC):
                    e.wait_ge(wn_h_ready, KC * layer + c + 1)
                    last = e.scalar_tensor_tensor(out=wq_l[:, c, QKV:W], in0=w_null[:, c, :],
                                                  scalar=g_in_sb[:, layer, c:c + 1],
                                                  in1=wq_h[:, c, QKV:W].bitcast(F32),
                                                  op0=ALU.mult, op1=ALU.subtract)
                last.then_inc(wq_ready, 1)

            def output_weights(layer):
                for c in range(OC):
                    e.wait_ge(wo_h_ready, OC * layer + c + 1)
                    last = e.tensor_tensor(wo_l[:, c, :], wo_raw[:, c, :], wo_h[:, c, :].bitcast(F32), ALU.subtract)
                last.then_inc(wo_ready, 1)

            def net_norm(pre, st, mv, ve, rstd, cen, gain, g):
                e.wait_ge(net_step, pre)
                e.bn_stats(ln_st[:, :], net).then_inc(net_step, 1)
                e.wait_ge(net_step, st)
                e.bn_aggr(ln_mv[:, :], ln_st[:, :]).then_inc(net_step, 1)
                e.wait_ge(net_step, mv)
                e.tensor_scalar(ln_ve[:, :], ln_mv[:, 1:2], EPS, None, ALU.add).then_inc(net_step, 1)
                e.wait_ge(net_step, rstd)
                e.tensor_scalar(net, net, ln_mv[:, 0:1], ln_rstd[:, :], ALU.subtract, ALU.mult).then_inc(net_step, 1)
                e.wait_ge(net_step, cen)
                e.tensor_tensor(net, net, g, ALU.mult).then_inc(net_step, 1)

            def net_silu(exp, plus, rec, silu):
                e.wait_ge(net_step, exp)
                e.tensor_scalar(net_e, net_e, 1.0, None, ALU.add).then_inc(net_step, 1)
                e.wait_ge(net_step, plus)
                e.reciprocal(net_e, net_e).then_inc(net_step, 1)
                e.wait_ge(net_step, rec)
                e.tensor_tensor(net, net, net_e, ALU.mult).then_inc(net_step, 1)

            def net_table():
                e.wait_ge(net_loaded, 16 * NET_LOADS)
                e.wait_ge(consts_ready, 4)
                e.tensor_copy(pos[:, :], pos_i[:, :]).then_inc(net_step, 1)
                e.wait_ge(net_step, POS)
                e.scalar_tensor_tensor(out=net, in0=w0_b, scalar=pos[:, :], in1=b0_b, op0=ALU.mult, op1=ALU.add)\
                    .then_inc(net_step, 1)
                net_norm(PRE1, ST1, MV1, VE1, RSTD1, CEN1, GAIN1, g_b[0])
                net_silu(EXP1, PLUS1, REC1, SILU1)
                e.wait_ge(net_step, MM1)
                e.tensor_tensor(net, bank_y[:, :], b1_b, ALU.add).then_inc(net_step, 1)
                net_norm(PRE2, ST2, MV2, VE2, RSTD2, CEN2, GAIN2, g_b[1])
                net_silu(EXP2, PLUS2, REC2, SILU2)
                e.wait_ge(net_step, MM2)
                e.memset(table_sb[:, P:2 * P], -BIG)
                e.tensor_scalar(table_sb[:, 0:P], bank_y[0:H, 0:P], b2_col[:, :], None, ALU.add).then_inc(net_step, 1)

            def ln_stats(m):
                wait(e, x_loaded, m, by=16)
                e.bn_stats(ln_st[:, :], x_in[:, :]).then_inc(ln_st_done, 1)
                wait(e, ln_st_done, m)
                e.nop(nofuse=True)
                e.bn_aggr(ln_mv[:, :], ln_st[:, :]).then_inc(ln_mv_done, 1)
                wait(e, ln_mv_done, m)
                e.tensor_scalar(ln_ve[:, :], ln_mv[:, 1:2], EPS, None, ALU.add).then_inc(ln_ve_done, 1)

            def ln_apply(m):
                wait(e, ln_rstd_done, m)
                wait(e, xt_psum, m, -1)
                e.tensor_scalar(xn[:, :], x_in[:, :], ln_mv[:, 0:1], ln_rstd[:, :], ALU.subtract, ALU.mult)\
                    .then_inc(xn_ready, 1)

            def split_xt(m):
                wait(e, xt_h_ready, m)
                e.tensor_tensor(xt_l[:, :, :], bank_t[:, :].rearrange("p (c t) -> p c t", c=KC),
                                xt_h[:, :, :].bitcast(F32), ALU.subtract).then_inc(xt_ready, 1)

            def q_sums(m, p):
                if m[0] == 0:
                    return
                first, n = PARTS[p]
                n += p == 2
                wait_in_layer1(e, squares_ready[p], m)
                e.reduce_sum(ss[:, first:first + n], squares[:, 0:n * DH].rearrange("p (h d) -> p h d", h=n), AX.X)\
                    .then_inc(q_sum[p], 1)
                wait_in_layer1(e, q_sum[p], m)
                e.tensor_scalar(ssc[:, first:first + n], ss[:, first:first + n], TINY, None, ALU.max)\
                    .then_inc(q_clamp[p], 1)

            def q_scale_out(m, p):
                first, n = PARTS[p]
                bank = bank_q[p % 2]
                if m[0] == 1:
                    wait_in_layer1(e, q_norm[p], m)
                    wait(e, qt_psum[1], m, -1)
                    last = e.tensor_tensor(
                        q_nat[:, first * DH:(first + n) * DH].rearrange("p (h d) -> p h d", h=n),
                        bank[:, 0:n * DH].rearrange("p (h d) -> p h d", h=n),
                        rnorm[:, first:first + n].unsqueeze(2).broadcast_to([P, n, DH]), ALU.mult)
                    if p < 2:
                        last.then_inc(q_done[p], 1)
                if p < 2:
                    return
                k0, v0, s0 = n * DH, (n + 1) * DH, (n + 2) * DH
                k2 = bank[:, k0:v0].unsqueeze(1).broadcast_to([P, 2, DH])
                wait(e, kt_psum, m, -1)
                if m[0] == 0:
                    wait(e, q_copied, m)
                    e.tensor_scalar(k_nat[:, :, :], k2, DH ** -0.5, None, ALU.mult)
                    e.scalar_tensor_tensor(out=nns_next[:, :], in0=bank[:, s0:s0 + H], scalar=-1.0,
                                           in1=null_bias_sb[:, 0, :], op0=ALU.mult, op1=ALU.subtract)\
                        .then_inc(nns_next_ready, 1)
                else:
                    e.scalar_tensor_tensor(out=k_nat[:, :, :], in0=k2, scalar=rnorm[:, H:H + 1],
                                           in1=k_mul[:, :].unsqueeze(1).broadcast_to([P, 2, DH]),
                                           op0=ALU.mult, op1=ALU.mult)
                    e.tensor_tensor(null_s[:, :], bank[:, s0:s0 + H], rnorm[:, 0:H], ALU.mult)\
                        .then_inc(null_s_done, 1)
                    wait_in_layer1(e, null_s_done, m)
                    e.scalar_tensor_tensor(out=nns_next[:, :], in0=null_s[:, :], scalar=-1.0,
                                           in1=null_bias_sb[:, 1, :], op0=ALU.mult, op1=ALU.subtract)\
                        .then_inc(nns_next_ready, 1)
                wait(e, v_ready, m, -1)
                e.tensor_tensor(v_raw[:, :], bank[:, v0:s0], null_v[:, :], ALU.subtract).then_inc(q_done[2], 1)

            def split_qt(m, half):
                wait(e, qt_h_ready[half], m)
                e.tensor_tensor(qt_l[:, 4 * half:4 * half + 4, :], bank_t[:, :].rearrange("p (c t) -> p c t", c=4),
                                qt_h[:, 4 * half:4 * half + 4, :].bitcast(F32), ALU.subtract)\
                    .then_inc(qt_ready[half], 1)

            def split_kt(m):
                wait(e, kt_h_ready, m)
                for half in range(2):
                    r = slice(half * DH, (half + 1) * DH)
                    last = e.tensor_tensor(kt_l[r, half, :], bank_t[r, 0:P], kt_h[r, half, :].bitcast(F32), ALU.subtract)
                last.then_inc(kt_ready, 1)

            def split_v(m):
                wait(e, v_h_ready, m)
                h2 = v_h[:, :].rearrange("p (a b d) -> p a b d", a=2, b=2)
                l2 = v_l[:, :].rearrange("p (a b d) -> p a b d", a=2, b=2)
                for half in range(2):
                    last = e.tensor_tensor(l2[:, half, half, :], v_raw[:, :], h2[:, half, half, :].bitcast(F32),
                                           ALU.subtract)
                last.then_inc(v_ready, 1)

            def take_null_scores(m):
                wait(e, nns_next_ready, m)
                e.tensor_copy(nns[:, :], nns_next[:, :]).then_inc(nns_ready, 1)

            def take_mask(m):
                if opens_layer(m):
                    e.wait_ge(rows_loaded, 16 * ROW_LOADS)
                wait(e, bias_ready[3], m, -1)
                e.tensor_scalar(mask_row[:, :], mask[:, m[0], m[1], :], -1.0, BIG, ALU.add, ALU.mult)\
                    .then_inc(mask_ready, 1)

            def scores(m, g):
                hs = slice(HG * g, HG * (g + 1))
                wait(e, s_psum[g], m)
                wait(e, bias_ready[g], m)
                wait(e, exp_ready[(g + 2) % G], m, -1 if g < 2 else 0)
                e.nop(nofuse=True)
                for j in range(HG):
                    h = HG * g + j
                    last = e.tensor_tensor_reduce(s_sb[:, g % 2, j, :], bank_s[g % 2][:, j * P:(j + 1) * P],
                                                  bias_g[:, g % 2, j, :], 1.0, LOWEST, ALU.add, ALU.max,
                                                  mx[:, h:h + 1])
                last.then_inc(s_ready[g], 1)
                wait(e, s_ready[g], m)
                if g == 0:
                    wait(e, nns_ready, m)
                e.scalar_tensor_tensor(out=neg_m[:, hs], in0=mx[:, hs], scalar=-1.0, in1=nns[:, hs],
                                       op0=ALU.mult, op1=ALU.min).then_inc(neg_m_ready[g], 1)
                wait(e, neg_m_ready[g], m)
                e.tensor_tensor(d_null[:, hs], neg_m[:, hs], nns[:, hs], ALU.subtract).then_inc(d_null_ready[g], 1)

            def sums(m, g):
                hs = slice(HG * g, HG * (g + 1))
                wait(e, exp_ready[g], m)
                e.tensor_tensor(den[:, hs], esum[:, hs], p_null[:, hs], ALU.add).then_inc(den_ready[g], 1)
                wait(e, den_ready[g], m)
                e.reciprocal(rden[:, hs], den[:, hs]).then_inc(rden_ready[g], 1)

            def split_pt(m, g):
                wait(e, pt_h_ready[g], m)
                e.tensor_tensor(pt_l[:, g % 2, :, :], bank_p[:, :].rearrange("p (h i) -> p h i", h=HG),
                                pt_h[:, g % 2, :, :].bitcast(F32), ALU.subtract).then_inc(pt_ready[g], 1)

            def split_ot(m, half):
                cs = slice(4 * half, 4 * half + 4)
                wait(e, ot_h_ready[half], m)
                e.scalar_tensor_tensor(out=ot_l[:, cs, :], in0=bank_o[:, :].rearrange("p (c t) -> p c t", c=4),
                                       scalar=null_v_col[:, :], in1=ot_h[:, cs, :].bitcast(F32),
                                       op0=ALU.add, op1=ALU.subtract).then_inc(ot_ready[half], 1)

            def y_stats(m):
                wait(e, wo_half[1], m)
                e.bn_stats(y_st[:, :], bank_y[:, :]).then_inc(y_st_done, 1)
                wait(e, y_st_done, m)
                e.nop(nofuse=True)
                e.bn_aggr(y_mv[:, :], y_st[:, :]).then_inc(y_mv_done, 1)
                wait(e, y_mv_done, m)
                e.tensor_scalar(y_ve[:, :], y_mv[:, 1:2], EPS, None, ALU.add).then_inc(y_ve_done, 1)
                e.scalar_tensor_tensor(out=y_t, in0=bank_y[:, :], scalar=y_mv[:, 0:1], in1=g_out_sb[:, m[0], :],
                                       op0=ALU.subtract, op1=ALU.mult).then_inc(y_out_of_psum, 1)

            def y_finish(m):
                wait(e, y_rstd_done, m)
                wait(e, y_out_of_psum, m)
                wait(e, res_loaded, m, by=16)
                wait(e, x_stored, m, -1, by=16)
                e.scalar_tensor_tensor(out=x_out, in0=y_t, scalar=y_rstd[:, :], in1=x_res[:, :],
                                       op0=ALU.mult, op1=ALU.add).then_inc(x_out_ready, 1)

            def step(at):
                m, after, prev, done, later = at(0), at(1), at(-1), at(-2), at(2)
                if m is not None:
                    take_null_scores(m)
                if prev is not None:
                    sums(prev, 3)
                if m is not None:
                    scores(m, 0)
                if prev is not None:
                    split_ot(prev, 0)
                if later is not None:
                    ln_stats(later)
                if done is not None:
                    y_finish(done)
                if m is not None:
                    sums(m, 0)
                if prev is not None:
                    split_pt(prev, 3)
                if after is not None:
                    q_sums(after, 0)
                if m is not None:
                    scores(m, 1)
                if later is not None:
                    ln_apply(later)
                if after is not None:
                    q_scale_out(after, 0)
                if m is not None:
                    sums(m, 1)
                    split_pt(m, 0)
                if after is not None:
                    q_sums(after, 1)
                if prev is not None:
                    split_ot(prev, 1)
                if m is not None:
                    split_v(m)
                    scores(m, 2)
                if after is not None:
                    q_scale_out(after, 1)
                if m is not None:
                    sums(m, 2)
                    split_pt(m, 1)
                if after is not None:
                    split_qt(after, 0)
                    q_sums(after, 2)
                if m is not None:
                    scores(m, 3)
                if after is not None:
                    q_scale_out(after, 2)
                    split_qt(after, 1)
                    take_mask(after)
                    split_kt(after)
                if m is not None:
                    split_pt(m, 2)
                if later is not None:
                    split_xt(later)
                if prev is not None:
                    y_stats(prev)

            def between(n):
                if n == B - 2:
                    null_columns(1, w1_sb[:, 0:2, :].rearrange("p c n -> p (c n)"))
                if n == B - 1:
                    project_weights(1)
                if n == B + 1:
                    output_weights(1)

            net_table()
            null_columns(0, y_out[:, :, :].rearrange("p a n -> p (a n)"))
            project_weights(0)
            output_weights(0)
            stream(e, step, between)

        @block.tensor
        def _(e):
            e.wait_ge(consts_ready, 4)

            def product(out, passes):
                for k, (a, b) in enumerate(passes):
                    last = e.matmul(out, a, b, start=(k == 0), stop=(k == len(passes) - 1))
                return last

            def net_transposes(silu, tp):
                e.wait_ge(net_step, silu)
                for c in range(KC):
                    last = e.transpose(bank_t[:, c * P:(c + 1) * P], net[:, c * P:(c + 1) * P], ident[:, :])
                last.then_inc(net_step, 1)

            net_transposes(SILU1, TP1)
            e.wait_ge(net_step, TCOPY1)
            product(bank_y[:, :], [(net_t[:, c, :], w1_sb[:, c, :]) for c in range(KC)]).then_inc(net_step, 1)
            net_transposes(SILU2, TP2)
            e.wait_ge(net_step, TCOPY2)
            product(bank_y[0:H, 0:P], [(w2_sb[:, c, :], net_t[:, c, :]) for c in range(KC)]).then_inc(net_step, 1)

            def transpose_x(m):
                wait(e, xn_ready, m)
                if opens_layer(m) and m[0] == 0:
                    e.wait_ge(net_step, TABLE)
                else:
                    wait(e, kt_ready, m, -1)
                for c in range(KC):
                    last = e.transpose(bank_t[:, c * P:(c + 1) * P], xn[:, c * P:(c + 1) * P], ident[:, :])
                last.then_inc(xt_psum, 1)

            def project(m, p):
                lo, hi = part_columns(p)
                if opens_layer(m) and p == 0:
                    e.wait_ge(wq_ready, m[0] + 1)
                if p == 0:
                    wait(e, xt_ready, m)
                    wait(e, q_done[2], m, -1)
                elif p == 1:
                    wait(e, q_done[1], m, -1)
                else:
                    wait(e, q_done[0], m)
                passes = []
                for c in range(KC):
                    passes += [(xt_h[:, c, :], wq_h[:, c, lo:hi]), (xt_h[:, c, :], wq_l[:, c, lo:hi]),
                               (xt_l[:, c, :], wq_h[:, c, lo:hi])]
                product(bank_q[p % 2][:, 0:hi - lo], passes).then_inc(q_psum[p], 1)

            def transpose_q(m, half):
                if half == 0:
                    wait(e, q_done[0], m)
                    wait(e, q_done[1], m)
                    wait(e, xt_ready, m)
                else:
                    wait(e, q_done[2], m)
                    wait(e, qt_ready[0], m)
                for c in range(4):
                    k = 4 * half + c
                    last = e.transpose(bank_t[:, c * P:(c + 1) * P], q_nat[:, k * P:(k + 1) * P], ident[:, :])
                last.then_inc(qt_psum[half], 1)

            def transpose_k(m):
                wait(e, qt_ready[1], m)
                e.transpose(bank_t[:, 0:P], k_nat[:, :, :].rearrange("p a d -> p (a d)"), ident[:, :])\
                    .then_inc(kt_psum, 1)

            def scores(m, g):
                if g % 2 == 0:
                    wait(e, qt_ready[g // 2], m)
                if g == 0:
                    wait(e, kt_ready, m)
                wait(e, s_ready[(g + 2) % G], m, -1 if g < 2 else 0)
                kh, kl = (t[:, :, :].rearrange("p a j -> p (a j)") for t in (kt_h, kt_l))
                for j in range(2):
                    c = 2 * g + j
                    last = product(bank_s[g % 2][:, j * 2 * P:(j + 1) * 2 * P],
                                   [(qt_h[:, c, :], kh), (qt_h[:, c, :], kl), (qt_l[:, c, :], kh)])
                last.then_inc(s_psum[g], 1)

            def transpose_p(m, g):
                wait(e, p_ready[g], m)
                wait(e, pt_ready[(g + 3) % G], m, -1 if g == 0 else 0)
                for j in range(HG):
                    last = e.transpose(bank_p[:, j * P:(j + 1) * P], p_sb[:, g % 2, j, :], ident[:, :])
                last.then_inc(pt_psum[g], 1)

            def attend(m, g):
                wait(e, pt_ready[g], m)
                if g == 0:
                    wait(e, v_ready, m)
                if g % 2 == 0:
                    wait(e, ot_ready[1 - g // 2], m, -1 if g == 0 else 0)
                passes = []
                for odd in range(2):
                    vh, vl = (t[:, odd * P:(odd + 1) * P] for t in (v_h, v_l))
                    ph, pl = (t[:, g % 2, odd::2, :] for t in (pt_h, pt_l))
                    passes += [(vh, ph), (vl, ph), (vh, pl)]
                o = bank_o[:, (g % 2) * 2 * P:(g % 2 + 1) * 2 * P].rearrange("p (c i) -> p c i", c=2)
                product(o, passes).then_inc(pv_psum[g], 1)

            def output(m, c0, c1):
                if opens_layer(m) and c0 == 0:
                    e.wait_ge(wo_ready, m[0] + 1)
                if c0 == 0:
                    wait(e, y_out_of_psum, m, -1)
                if c0 % 4 == 0:
                    wait(e, ot_ready[c0 // 4], m)
                for c in range(c0, c1):
                    for k, (a, b) in enumerate(((ot_h, wo_h), (ot_h, wo_l), (ot_l, wo_h))):
                        last = e.matmul(bank_y[:, :], a[:, c, :], b[:, c, :], start=(c == 0 and k == 0),
                                        stop=(c == OC - 1 and k == 2))
                if c1 % 4 == 0:
                    last.then_inc(wo_half[c1 // 4 - 1], 1)

            def step(at):
                m, after, prev, later = at(0), at(1), at(-1), at(2)
                if m is not None:
                    scores(m, 0)
                if after is not None:
                    project(after, 0)
                if prev is not None:
                    transpose_p(prev, 3)
                    attend(prev, 2)
                if m is not None:
                    scores(m, 1)
                if prev is not None:
                    output(prev, 0, 2)
                if m is not None:
                    transpose_p(m, 0)
                if after is not None:
                    project(after, 1)
                if prev is not None:
                    attend(prev, 3)
                if m is not None:
                    scores(m, 2)
                if after is not None:
                    project(after, 2)
                if m is not None:
                    transpose_p(m, 1)
                if after is not None:
                    transpose_q(after, 0)
                if prev is not None:
                    output(prev, 2, 4)
                if m is not None:
                    attend(m, 0)
                    scores(m, 3)
                if after is not None:
                    transpose_q(after, 1)
                if prev is not None:
                    output(prev, 4, 6)
                if after is not None:
                    transpose_k(after)
                if m is not None:
                    transpose_p(m, 2)
                if prev is not None:
                    output(prev, 6, 8)
                if later is not None:
                    transpose_x(later)
                if m is not None:
                    attend(m, 1)

            stream(e, step)


_INS = ["x", "fside_16xSxS_0", "cond_64", "mask_BxS_bk0", "mask_BxS_bf1",
        "L0_cond_g_in", "L0_cond_null_attn_bias", "L0_cond_Wq", "L0_cond_Wkv", "L0_cond_Wo", "L0_cond_g_out",
        "L1_cond_g_norm", "L1_cond_Wq", "L1_cond_Wkv", "L1_cond_q_scale", "L1_cond_k_scale",
        "L1_cond_null_attn_bias", "L1_cond_w0", "L1_cond_b0", "L1_cond_g0", "L1_cond_w1", "L1_cond_b1",
        "L1_cond_g1", "L1_cond_w2", "L1_cond_b2", "L1_cond_Wout", "L1_cond_g_out"]


def kernel(**inputs):
    import numpy as _np
    import concourse.bacc as _bacc
    from concourse import mybir as _mybir
    from concourse.bass_utils import run_bass_kernel_spmd as _run

    nc = _bacc.Bacc("TRN2", target_bir_lowering=False, num_devices=1)
    arrays, a = {}, {}
    for name in _INS:
        v = _np.ascontiguousarray(inputs[name])
        arrays[f"in_{name}"] = v
        a[name] = nc.dram_tensor(f"in_{name}", v.shape, _mybir.dt.from_np(v.dtype), kind="ExternalInput").ap()
    out = nc.dram_tensor("out_x", (B, P, D), F32, kind="ExternalOutput").ap()
    build(nc, a["x"], a["fside_16xSxS_0"], a["cond_64"], a["mask_BxS_bk0"], a["mask_BxS_bf1"],
          [a["L0_cond_g_in"], a["L1_cond_g_norm"]],
          [a["L0_cond_null_attn_bias"], a["L1_cond_null_attn_bias"]],
          [a["L0_cond_Wq"], a["L1_cond_Wq"]], [a["L0_cond_Wkv"], a["L1_cond_Wkv"]],
          [a["L0_cond_Wo"], a["L1_cond_Wout"]], [a["L0_cond_g_out"], a["L1_cond_g_out"]],
          a["L1_cond_q_scale"], a["L1_cond_k_scale"], a["L1_cond_w0"], a["L1_cond_b0"], a["L1_cond_g0"],
          a["L1_cond_w1"], a["L1_cond_b1"], a["L1_cond_g1"], a["L1_cond_w2"], a["L1_cond_b2"], out)
    r = _run(nc, [arrays], core_ids=[0])
    return r.results[0]["out_x"]
```

```python
from contextlib import ExitStack

import concourse.bass as bass
from concourse import mybir

ALU = mybir.AluOpType
ACT = mybir.ActivationFunctionType
AX = mybir.AxisListType
F32 = mybir.dt.float32
F32R = mybir.dt.float32r
I32 = mybir.dt.int32
U8 = mybir.dt.uint8

P = 128
B = 32
D = 512
H = 16
DH = 64
INNER = H * DH
LAYERS = 2
N = LAYERS * B
KC = D // P
OC = INNER // P
QKV = INNER + 2 * DH
W = QKV + H
G = 4
HG = H // G
PARTS = [(0, 6), (6, 6), (12, 4)]
EPS = 1e-5
TINY = 1e-24
BIG = 1e38
LOWEST = -3.4e38
FIRST, LAST = 3, B - 4


def part_columns(p):
    first, count = PARTS[p]
    return first * DH, (W if p == len(PARTS) - 1 else (first + count) * DH)


def count(m, d=0):
    layer, b = m
    return b + (layer * B + 1 + d)


def wait(e, sem, m, d=0, by=1):
    value = count(m, d) * by
    if not (isinstance(value, int) and value <= 0):
        e.wait_ge(sem, value)


def wait_in_layer1(e, sem, m, d=0):
    value = m[1] + (1 + d)
    if not (isinstance(value, int) and value <= 0):
        e.wait_ge(sem, value)


def step_count(at):
    return count(at(3)) if at(3) is not None else count(at(-1), 4)


def opens_layer(m):
    return isinstance(m[1], int) and m[1] == 0


def stream(e, step, between=None):
    def straight(first, last):
        for n in range(first, last):
            if between:
                between(n)
            step(lambda d, n=n: ((n + d) // B, (n + d) % B) if 0 <= n + d < N else None)

    straight(-3, FIRST)
    for layer in range(LAYERS):
        with e.Fori(FIRST, LAST + 1) as i:
            step(lambda d: (layer, i + d))
        straight(layer * B + LAST + 1, (layer + 1) * B + FIRST if layer + 1 < LAYERS else N + 1)


def build(nc, x, bias0, cond, mask0, mask1, g_in, null_bias, wq, wkv, wo, g_out, q_scale, k_scale,
          w0, b0, g0, w1, b1, g1, w2, b2, out):
    x_mid = nc.dram_tensor("x_mid", (B, P, D), F32, kind="Internal").ap()
    table = nc.dram_tensor("bias_table", (H, P, 2 * P), F32, kind="Internal").ap()
    x_of = [x, x_mid]
    out_of = [x_mid, out]

    with ExitStack() as ctx:
        def sb(name, shape, dt=F32):
            return ctx.enter_context(nc.sbuf_tensor(name, shape, dt))

        def psum(name):
            return ctx.enter_context(nc.psum_tensor(name, [P, 512], F32))

        def sem(name):
            return ctx.enter_context(nc.semaphore(name))

        def sems(name, n):
            return [sem(f"{name}{i}") for i in range(n)]

        wq_h = sb("wq_h", [P, KC, W], F32R)
        wq_l = sb("wq_l", [P, KC, W], F32R)
        wo_h = sb("wo_h", [P, OC, D], F32R)
        wo_l = sb("wo_l", [P, OC, D], F32R)
        wq_raw = sb("wq_raw", [P, KC, QKV])
        wo_raw = sb("wo_raw", [P, OC, D])
        w_null = sb("w_null", [P, KC, H])
        bias = sb("bias", [P, LAYERS, H, P])
        mask = sb("mask", [P, LAYERS, B, P], U8)
        g_in_sb = sb("g_in_sb", [P, LAYERS, KC])
        g_out_sb = sb("g_out_sb", [P, LAYERS, D])
        null_bias_sb = sb("null_bias_sb", [P, LAYERS, H])
        null_k = sb("null_k", [P, DH])
        null_kn = sb("null_kn", [P, LAYERS, DH])
        null_v = sb("null_v", [P, DH])
        null_v_col = sb("null_v_col", [P, 1])
        qs = sb("qs", [P, DH])
        k_mul = sb("k_mul", [P, DH])
        nk_sq = sb("nk_sq", [P, DH])
        nk_ss = sb("nk_ss", [P, 2])
        ident = sb("ident", [P, P])
        minus_half = sb("minus_half", [P, 8])
        x_in = sb("x_in", [P, D])
        x_res = sb("x_res", [P, D])
        xn = sb("xn", [P, D])
        xt_h = sb("xt_h", [P, KC, P], F32R)
        xt_l = sb("xt_l", [P, KC, P], F32R)
        q_nat = sb("q_nat", [P, INNER])
        squares = sb("squares", [P, 6 * DH])
        k_nat = sb("k_nat", [P, 2, DH])
        v_raw = sb("v_raw", [P, DH])
        moments = sb("moments", [P, 2, 6])
        mean_var = sb("mean_var", [P, 2, 2])
        var_eps = sb("var_eps", [P, 2])
        rstd = sb("rstd", [P, 2])
        ss = sb("ss", [P, H + 1])
        ssc = sb("ssc", [P, H + 1])
        rnorm = sb("rnorm", [P, H + 1])
        null_s = sb("null_s", [P, H])
        nns_next = sb("nns_next", [P, H])
        nns = sb("nns", [P, H])
        qt_h = sb("qt_h", [P, OC, P], F32R)
        qt_l = sb("qt_l", [P, OC, P], F32R)
        kt_h = sb("kt_h", [P, 2, P], F32R)
        kt_l = sb("kt_l", [P, 2, P], F32R)
        v_h = sb("v_h", [P, 2 * P], F32R)
        v_l = sb("v_l", [P, 2 * P], F32R)
        mask_row = sb("mask_row", [P, P])
        bias_g = sb("bias_g", [P, 2, HG, P])
        s_sb = sb("s_sb", [P, 2, HG, P + 1])
        mx = sb("mx", [P, H])
        neg_m = sb("neg_m", [P, H])
        esum = sb("esum", [P, H])
        rden = sb("rden", [P, H])
        p_raw = sb("p_raw", [P, 2, HG, P + 1])
        p_sb = sb("p_sb", [P, 2, HG, P])
        pt_h = sb("pt_h", [P, 2, HG, P], F32R)
        pt_l = sb("pt_l", [P, 2, HG, P], F32R)
        ot_h = sb("ot_h", [P, OC, P], F32R)
        ot_l = sb("ot_l", [P, OC, P], F32R)
        y_out = sb("y_out", [P, 2, D])
        y_t, x_out = y_out[:, 0, :], y_out[:, 1, :]
        w1_sb = sb("w1_sb", [P, KC, D])
        w2_sb = sb("w2_sb", [P, KC, H])
        b2_col = sb("b2_col", [H, 1])
        pos_i = sb("pos_i", [P, 1], I32)
        pos = sb("pos", [P, 1])
        table_sb = squares[0:H, 0:2 * P]
        flat = lambda t: t[:, :, :, :].rearrange("p a h j -> p a (h j)")
        w0_b, b0_b = flat(p_raw)[:, 0, 0:D], flat(p_raw)[:, 1, 0:D]
        g_b, b1_b = [flat(p_sb)[:, 0, :], flat(p_sb)[:, 1, :]], q_nat[:, 0:D]
        net = flat(s_sb)[:, 0, 0:D]
        net_t = flat(s_sb)[:, 1, 0:D].rearrange("p (c t) -> p c t", c=KC)
        net_e = q_nat[:, D:2 * D]

        bank_s = [psum("bank_s0"), psum("bank_s1")]
        bank_p = psum("bank_p")
        bank_q = [psum("bank_q0"), psum("bank_q1")]
        bank_o = psum("bank_o")
        bank_t = psum("bank_t")
        bank_y = psum("bank_y")

        wq_loaded = sem("wq_loaded")
        wo_loaded = sem("wo_loaded")
        small_loaded = sem("small_loaded")
        rows_loaded = sem("rows_loaded")
        bias0_loaded = sem("bias0_loaded")
        net_loaded = sem("net_loaded")
        table_stored = sem("table_stored")
        bias1_loaded = sem("bias1_loaded")
        consts_ready = sem("consts_ready")
        zeros_ready = sem("zeros_ready")
        causal_ready = sem("causal_ready")
        nk_step = sem("nk_step")
        null_prod = sem("null_prod")
        null_ready = sem("null_ready")
        wq_h_ready = sem("wq_h_ready")
        wn_h_ready = sem("wn_h_ready")
        wq_ready = sem("wq_ready")
        wo_h_ready = sem("wo_h_ready")
        wo_ready = sem("wo_ready")
        net_step = sem("net_step")
        x_loaded = sem("x_loaded")
        res_loaded = sem("res_loaded")
        x_stored = sem("x_stored")
        x_moments = sem("x_moments")
        y_moments = sem("y_moments")
        mean_var_done = sem("mean_var_done")
        var_eps_done = sem("var_eps_done")
        rstd_done = sem("rstd_done")
        xn_ready = sem("xn_ready")
        xt_psum = sem("xt_psum")
        xt_h_ready = sem("xt_h_ready")
        xt_ready = sem("xt_ready")
        q_psum = sems("q_psum", 3)
        q_copied = sem("q_copied")
        squares_ready = sems("squares_ready", 3)
        q_sum = sems("q_sum", 3)
        q_clamp = sems("q_clamp", 3)
        q_norm = sems("q_norm", 3)
        q_done = sems("q_done", 3)
        null_s_done = sem("null_s_done")
        nns_next_ready = sem("nns_next_ready")
        nns_ready = sem("nns_ready")
        qt_psum = sems("qt_psum", 2)
        qt_h_ready = sems("qt_h_ready", 2)
        qt_ready = sems("qt_ready", 2)
        kt_psum = sem("kt_psum")
        kt_h_ready = sem("kt_h_ready")
        kt_ready = sem("kt_ready")
        v_h_ready = sem("v_h_ready")
        v_ready = sem("v_ready")
        mask_ready = sem("mask_ready")
        bias_ready = sems("bias_ready", G)
        s_psum = sems("s_psum", G)
        s_ready = sems("s_ready", G)
        neg_m_ready = sems("neg_m_ready", G)
        exp_ready = sems("exp_ready", G)
        rden_ready = sems("rden_ready", G)
        p_ready = sems("p_ready", G)
        pt_psum = sems("pt_psum", G)
        pt_h_ready = sems("pt_h_ready", G)
        pt_ready = sems("pt_ready", G)
        pv_psum = sems("pv_psum", G)
        ot_h_ready = sems("ot_h_ready", 2)
        ot_ready = sems("ot_ready", 2)
        wo_half = sems("wo_half", 2)
        y_out_of_psum = sem("y_out_of_psum")
        x_out_ready = sem("x_out_ready")

        WQ_LOADS, WO_LOADS = 2, 1
        SMALL_LOADS = 6 + 2 * LAYERS
        ROW_LOADS = 2 * LAYERS
        NET_LOADS = 8
        (POS, PRE1, ST1, MV1, VE1, RSTD1, CEN1, GAIN1, EXP1, PLUS1, REC1, SILU1, TP1, TCOPY1,
         MM1, PRE2, ST2, MV2, VE2, RSTD2, CEN2, GAIN2, EXP2, PLUS2, REC2, SILU2, TP2, TCOPY2,
         MM2, TABLE) = range(1, 31)

        block = ctx.enter_context(nc.Block())

        @block.sync
        def _(e):
            def load_wq(layer):
                e.dma_start(wq_raw[:, :, 0:INNER], wq[layer].rearrange("(c p) n -> p c n", p=P)).then_inc(wq_loaded, 16)
                e.dma_start(wq_raw[:, :, INNER:QKV], wkv[layer].rearrange("(c p) n -> p c n", p=P)).then_inc(wq_loaded, 16)

            def load_wo(layer):
                e.dma_start(wo_raw[:, :, :], wo[layer].rearrange("(c p) n -> p c n", p=P)).then_inc(wo_loaded, 16)

            def row(v):
                return v.rearrange("(a n) -> a n", a=1)

            def small(dst, src, **how):
                e.dma_start(dst, src, **how).then_inc(small_loaded, 16)

            small(null_k[:, :], cond[0:1, :].broadcast_to([P, DH]))
            small(qs[:, :], row(q_scale).broadcast_to([P, DH]))
            small(k_mul[:, :], row(k_scale).broadcast_to([P, DH]))
            small(null_v[:, :], cond[1:2, :].broadcast_to([P, DH]))
            for half in range(2):
                small(null_v_col[half * DH:(half + 1) * DH, :], cond[1:2, :].rearrange("a d -> d a"))
            for layer in range(LAYERS):
                small(g_in_sb[:, layer, :], g_in[layer].rearrange("(c p) -> p c", p=P), allow_slow_non_contiguous=True)
                small(null_bias_sb[:, layer, :], row(null_bias[layer]).broadcast_to([P, H]))
            load_wq(0)
            for layer in range(LAYERS):
                e.dma_start(g_out_sb[:, layer, :], row(g_out[layer]).broadcast_to([P, D])).then_inc(rows_loaded, 16)
                m = (mask0, mask1)[layer].rearrange("(a b) s -> a b s", a=1)
                e.dma_start(mask[:, layer, :, :], m.broadcast_to([P, B, P])).then_inc(rows_loaded, 16)
            e.dma_start(bias[:, 0, :, :], bias0.rearrange("h i j -> i h j")).then_inc(bias0_loaded, 16)
            load_wo(0)

            def step(at):
                if (m := at(-1)) is not None:
                    wait(e, x_out_ready, m, -1)
                    e.dma_start(x_res[:, :], x_of[m[0]][m[1]]).then_inc(res_loaded, 16)
                if (m := at(3)) is not None:
                    wait(e, xn_ready, m, -1)
                    if m[0] == 1:
                        e.wait_ge(x_stored, (m[1] + 1) * 16)
                    e.dma_start(x_in[:, :], x_of[m[0]][m[1]]).then_inc(x_loaded, 16)
                if (m := at(-1)) is not None:
                    wait(e, x_out_ready, m)
                    e.dma_start(out_of[m[0]][m[1]], x_out).then_inc(x_stored, 16)

            def between(n):
                if n == -1:
                    e.wait_ge(wq_ready, 1)
                    load_wq(1)
                if n == 0:
                    e.wait_ge(wo_ready, 2)
                    load_wo(1)
                    e.wait_ge(net_step, TABLE)
                    e.dma_start(table, table_sb.unsqueeze(1).broadcast_to([H, P, 2 * P])).then_inc(table_stored, 16)
                if n == 1:
                    e.wait_ge(table_stored, 16)
                    shifted = bass.AP(table.tensor, P - 1, [[2 * P - 1, P], [2 * P * P, H], [1, P]])
                    e.dma_start(bias[:, 1, :, :], shifted)\
                        .then_inc(bias1_loaded, 16)

            stream(e, step, between)
            e.wait_ge(x_stored, 16 * N)

        @block.gpsimd
        def _(e):
            e.memset(ident[:, :], 0.0).then_inc(consts_ready, 1)
            e.memset(minus_half[:, :], -0.5).then_inc(consts_ready, 1)
            e.iota(pos_i[:, :], pattern=[[0, 1]], base=P - 1, channel_multiplier=-1).then_inc(consts_ready, 1)
            e.wait_ge(consts_ready, 3)
            e.affine_select(out=ident[:, :], in_=ident[:, :], compare_op=ALU.not_equal, fill=1.0, base=0,
                            pattern=[[-1, P]], channel_multiplier=1).then_inc(consts_ready, 1)
            e.wait_ge(nk_step, 4)
            e.tensor_tensor(nk_ss[:, 1:2], nk_ss[:, 0:1], minus_half[:, 0:1], ALU.pow).then_inc(nk_step, 1)
            for ve, done in ((VE1, RSTD1), (VE2, RSTD2)):
                e.wait_ge(net_step, ve)
                e.tensor_tensor(rstd[:, 0:1], var_eps[:, 0:1], minus_half[:, 0:1], ALU.pow).then_inc(net_step, 1)
            e.wait_ge(bias0_loaded, 16)
            e.affine_select(out=bias[:, 0, :, :], in_=bias[:, 0, :, :], compare_op=ALU.is_ge, fill=-BIG, base=0,
                            pattern=[[0, H], [-1, P]], channel_multiplier=1).then_inc(causal_ready, 1)

            def masked_bias(m, g):
                if opens_layer(m) and g == 0:
                    if m[0] == 0:
                        e.wait_ge(causal_ready, 1)
                    else:
                        e.wait_ge(bias1_loaded, 16)
                if g == 0:
                    wait(e, mask_ready, m)
                wait(e, s_ready[(g + 2) % G], m, -1 if g < 2 else 0)
                e.tensor_tensor(bias_g[:, g % 2, :, :], bias[:, m[0], HG * g:HG * (g + 1), :],
                                mask_row[:, :].unsqueeze(1).broadcast_to([P, HG, P]), ALU.add)\
                    .then_inc(bias_ready[g], 1)

            def normalise(m, g):
                wait(e, rden_ready[g], m)
                wait(e, pt_psum[(g + 2) % G], m, -1 if g < 2 else 0)
                r = rden[:, HG * g:HG * (g + 1)].unsqueeze(2).broadcast_to([P, HG, P])
                e.tensor_tensor(p_sb[:, g % 2, :, :], p_raw[:, g % 2, :, 0:P], r, ALU.mult).then_inc(p_ready[g], 1)

            def norms(m, p):
                if m[0] == 0:
                    return
                first, n = PARTS[p]
                n += p == 2
                wait_in_layer1(e, q_sum[p], m)
                e.nop(nofuse=True)
                e.tensor_scalar(ssc[:, first:first + n], ss[:, first:first + n], TINY, None, ALU.max)\
                    .then_inc(q_clamp[p], 1)
                wait_in_layer1(e, q_clamp[p], m)
                e.tensor_tensor(rnorm[:, first:first + n], ssc[:, first:first + n], minus_half[:, 0:n], ALU.pow)\
                    .then_inc(q_norm[p], 1)

            def inverse_deviations(at):
                e.wait_ge(var_eps_done, step_count(at))
                e.tensor_tensor(rstd[:, :], var_eps[:, :], minus_half[:, 0:2], ALU.pow).then_inc(rstd_done, 1)

            def step(at):
                def on(d, stage, *which):
                    if at(d) is not None:
                        stage(at(d), *which)

                on(0, masked_bias, 2)
                on(0, masked_bias, 3)
                on(0, normalise, 0)
                on(1, masked_bias, 0)
                on(1, norms, 0)
                on(0, normalise, 1)
                on(1, masked_bias, 1)
                on(0, normalise, 2)
                on(1, norms, 1)
                inverse_deviations(at)
                on(0, normalise, 3)
                on(1, norms, 2)
            stream(e, step)

        @block.scalar
        def _(e):
            def net_load(dst, src):
                e.dma_start(dst, src).then_inc(net_loaded, 16)

            def row(v):
                return v.rearrange("(a n) -> a n", a=1).broadcast_to([P, D])

            net_load(w0_b, w0.broadcast_to([P, D]))
            net_load(b0_b, row(b0))
            net_load(g_b[0], row(g0))
            net_load(g_b[1], row(g1))
            net_load(b1_b, row(b1))
            net_load(w1_sb[:, :, :], w1.rearrange("(c p) n -> p c n", p=P))
            net_load(w2_sb[:, :, :], w2.rearrange("(c p) n -> p c n", p=P))
            net_load(b2_col[:, :], b2.rearrange("(h a) -> h a", a=1))

            def net_silu(gain, exp):
                e.wait_ge(net_step, gain)
                e.activation(net_e, net, ACT.Exp, scale=-1.0).then_inc(net_step, 1)

            def net_copy(tp, copy):
                e.wait_ge(net_step, tp)
                e.activation(net_t, bank_t[:, :].rearrange("p (c t) -> p c t", c=KC), ACT.Copy).then_inc(net_step, 1)

            def project_weights(layer):
                e.wait_ge(wq_loaded, 16 * WQ_LOADS * (layer + 1))
                e.wait_ge(small_loaded, 16 * SMALL_LOADS)
                if layer:
                    e.wait_ge(q_psum[2], B)
                for c in range(KC):
                    e.activation(wq_h[:, c, 0:QKV], wq_raw[:, c, :], ACT.Copy, scale=g_in_sb[:, layer, c:c + 1])\
                        .then_inc(wq_h_ready, 1)
                e.wait_ge(null_ready, KC * (layer + 1))
                for c in range(KC):
                    e.activation(wq_h[:, c, QKV:W], w_null[:, c, :], ACT.Copy, scale=g_in_sb[:, layer, c:c + 1])\
                        .then_inc(wn_h_ready, 1)

            def output_weights(layer, half):
                e.wait_ge(wo_loaded, 16 * WO_LOADS * (layer + 1))
                if layer:
                    e.wait_ge(wo_half[half], B)
                for c in range(4 * half, 4 * half + 4):
                    e.activation(wo_h[:, c, :], wo_raw[:, c, :], ACT.Copy).then_inc(wo_h_ready, 1)

            def split_xt(m):
                wait(e, xt_psum, m)
                wait(e, q_psum[2], m, -1)
                e.activation(xt_h[:, :, :], bank_t[:, :].rearrange("p (c t) -> p c t", c=KC), ACT.Copy)\
                    .then_inc(xt_h_ready, 1)

            def q_out(m, p):
                first, n = PARTS[p]
                wait(e, q_psum[p], m)
                if m[0] == 0:
                    wait(e, qt_psum[1], m, -1)
                    e.activation(q_nat[:, first * DH:(first + n) * DH], bank_q[p % 2][:, 0:n * DH], ACT.Copy)\
                        .then_inc(q_done[p] if p < 2 else q_copied, 1)
                else:
                    n += p == 2
                    wait_in_layer1(e, q_sum[(p + 2) % 3], m, 0 if p else -1)
                    e.activation(squares[:, 0:n * DH], bank_q[p % 2][:, 0:n * DH], ACT.Square)\
                        .then_inc(squares_ready[p], 1)

            def split_qt(m, half):
                wait(e, qt_psum[half], m)
                wait(e, s_psum[2 * half + 1], m, -1)
                e.activation(qt_h[:, 4 * half:4 * half + 4, :], bank_t[:, :].rearrange("p (c t) -> p c t", c=4),
                             ACT.Copy).then_inc(qt_h_ready[half], 1)

            def split_kt(m):
                wait(e, kt_psum, m)
                wait(e, s_psum[3], m, -1)
                for half in range(2):
                    r = slice(half * DH, (half + 1) * DH)
                    last = e.activation(kt_h[r, half, :], bank_t[r, 0:P], ACT.Copy)
                last.then_inc(kt_h_ready, 1)

            def split_v(m):
                wait(e, q_done[2], m)
                wait(e, pv_psum[3], m, -1)
                v2 = v_h[:, 0:2 * P].rearrange("p (a b d) -> p a b d", a=2, b=2)
                for half in range(2):
                    last = e.activation(v2[:, half, half, :], v_raw[:, :], ACT.Copy)
                last.then_inc(v_h_ready, 1)

            def exps(m, g):
                wait(e, neg_m_ready[g], m)
                wait(e, p_ready[(g + 2) % G], m, -1 if g < 2 else 0)
                for j in range(HG):
                    h = HG * g + j
                    last = e.activation(p_raw[:, g % 2, j, :], s_sb[:, g % 2, j, :], ACT.Exp, bias=neg_m[:, h:h + 1],
                                        accum_out=esum[:, h:h + 1])
                last.then_inc(exp_ready[g], 1)

            def split_pt(m, g):
                wait(e, pt_psum[g], m)
                wait(e, pv_psum[(g + 2) % G], m, -1 if g < 2 else 0)
                e.activation(pt_h[:, g % 2, :, :], bank_p[:, :].rearrange("p (h i) -> p h i", h=HG), ACT.Copy)\
                    .then_inc(pt_h_ready[g], 1)

            def split_ot(m, half):
                wait(e, pv_psum[2 * half + 1], m)
                wait(e, wo_half[half], m, -1)
                e.activation(ot_h[:, 4 * half:4 * half + 4, :], bank_o[:, :].rearrange("p (c t) -> p c t", c=4),
                             ACT.Identity, bias=null_v_col[:, :]).then_inc(ot_h_ready[half], 1)

            def step(at):
                def on(d, stage, *which):
                    if at(d) is not None:
                        stage(at(d), *which)

                on(1, split_xt)
                on(0, exps, 0)
                on(0, exps, 1)
                on(1, q_out, 0)
                on(-1, split_ot, 1)
                on(0, exps, 2)
                on(1, q_out, 1)
                on(0, split_v)
                on(0, split_pt, 0)
                on(0, exps, 3)
                on(1, q_out, 2)
                on(0, split_pt, 1)
                on(1, split_qt, 0)
                on(0, split_pt, 2)
                on(0, split_ot, 0)
                on(1, split_qt, 1)
                on(0, split_pt, 3)
                on(1, split_kt)

            def between(n):
                if n == B - 1:
                    project_weights(1)
                if n in (B, B + 1):
                    output_weights(1, n - B)

            net_silu(GAIN1, EXP1)
            net_copy(TP1, TCOPY1)
            net_silu(GAIN2, EXP2)
            net_copy(TP2, TCOPY2)
            project_weights(0)
            output_weights(0, 0)
            output_weights(0, 1)
            stream(e, step, between)

        @block.vector
        def _(e):
            for t in (kt_h, kt_l):
                e.memset(t[:, :, :].bitcast(F32), 0.0)
            e.memset(mean_var[:, :, :], 0.0)
            e.memset(v_h[:, :].bitcast(F32), 0.0)
            e.memset(v_l[:, :].bitcast(F32), 0.0).then_inc(zeros_ready, 1)
            e.wait_ge(zeros_ready, 1)

            e.wait_ge(small_loaded, 16 * SMALL_LOADS)
            e.tensor_scalar(null_kn[:, 0, :], null_k[:, :], DH ** -0.5, None, ALU.mult)
            e.tensor_tensor(nk_sq[:, :], null_k[:, :], null_k[:, :], ALU.mult).then_inc(nk_step, 1)
            e.scalar_tensor_tensor(out=k_mul[:, :], in0=k_mul[:, :], scalar=8.0, in1=qs[:, :], op0=ALU.mult,
                                   op1=ALU.mult).then_inc(nk_step, 1)
            e.wait_ge(nk_step, 2)
            e.reduce_sum(nk_ss[:, 1:2], nk_sq[:, :], AX.X).then_inc(nk_step, 1)
            e.wait_ge(nk_step, 3)
            e.tensor_scalar(nk_ss[:, 0:1], nk_ss[:, 1:2], TINY, None, ALU.max).then_inc(nk_step, 1)
            e.wait_ge(consts_ready, 4)
            e.wait_ge(nk_step, 5)
            e.scalar_tensor_tensor(out=null_kn[:, 1, :], in0=null_k[:, :], scalar=nk_ss[:, 1:2], in1=k_mul[:, :],
                                   op0=ALU.mult, op1=ALU.mult).then_inc(nk_step, 1)

            def null_columns(layer, scratch):
                e.wait_ge(nk_step, 6)
                e.wait_ge(wq_loaded, 16 * WQ_LOADS * (layer + 1))
                s = scratch.rearrange("p (h d) -> p h d", h=H)
                for c in range(KC):
                    k = KC * layer + c
                    if k:
                        e.wait_ge(null_ready, k)
                    e.tensor_tensor(s, wq_raw[:, c, 0:INNER].rearrange("p (h d) -> p h d", h=H),
                                    null_kn[:, layer, :].unsqueeze(1).broadcast_to([P, H, DH]), ALU.mult)\
                        .then_inc(null_prod, 1)
                    e.wait_ge(null_prod, k + 1)
                    if layer:
                        e.wait_ge(wn_h_ready, KC)
                    e.reduce_sum(w_null[:, c, :], s, AX.X).then_inc(null_ready, 1)

            def project_weights(layer):
                if layer:
                    e.wait_ge(q_psum[2], B)
                for c in range(KC):
                    e.wait_ge(wq_h_ready, KC * layer + c + 1)
                    e.scalar_tensor_tensor(out=wq_l[:, c, 0:QKV], in0=wq_raw[:, c, :],
                                           scalar=g_in_sb[:, layer, c:c + 1], in1=wq_h[:, c, 0:QKV].bitcast(F32),
                                           op0=ALU.mult, op1=ALU.subtract)
                for c in range(KC):
                    e.wait_ge(wn_h_ready, KC * layer + c + 1)
                    last = e.scalar_tensor_tensor(out=wq_l[:, c, QKV:W], in0=w_null[:, c, :],
                                                  scalar=g_in_sb[:, layer, c:c + 1],
                                                  in1=wq_h[:, c, QKV:W].bitcast(F32),
                                                  op0=ALU.mult, op1=ALU.subtract)
                last.then_inc(wq_ready, 1)

            def output_weights(layer, half):
                for c in range(4 * half, 4 * half + 4):
                    e.wait_ge(wo_h_ready, OC * layer + c + 1)
                    last = e.tensor_tensor(wo_l[:, c, :], wo_raw[:, c, :], wo_h[:, c, :].bitcast(F32), ALU.subtract)
                last.then_inc(wo_ready, 1)

            def net_norm(pre, st, mv, ve, rstd_step, cen, gain, g):
                e.wait_ge(net_step, pre)
                e.bn_stats(moments[:, 0, :], net).then_inc(net_step, 1)
                e.wait_ge(net_step, st)
                e.bn_aggr(mean_var[:, 0, :], moments[:, 0, :]).then_inc(net_step, 1)
                e.wait_ge(net_step, mv)
                e.tensor_scalar(var_eps[:, 0:1], mean_var[:, 0, 1:2], EPS, None, ALU.add).then_inc(net_step, 1)
                e.wait_ge(net_step, rstd_step)
                e.tensor_scalar(net, net, mean_var[:, 0, 0:1], rstd[:, 0:1], ALU.subtract, ALU.mult)\
                    .then_inc(net_step, 1)
                e.wait_ge(net_step, cen)
                e.tensor_tensor(net, net, g, ALU.mult).then_inc(net_step, 1)

            def net_silu(exp, plus, rec, silu):
                e.wait_ge(net_step, exp)
                e.tensor_scalar(net_e, net_e, 1.0, None, ALU.add).then_inc(net_step, 1)
                e.wait_ge(net_step, plus)
                e.reciprocal(net_e, net_e).then_inc(net_step, 1)
                e.wait_ge(net_step, rec)
                e.tensor_tensor(net, net, net_e, ALU.mult).then_inc(net_step, 1)

            def net_table():
                e.wait_ge(net_loaded, 16 * NET_LOADS)
                e.wait_ge(consts_ready, 4)
                e.tensor_copy(pos[:, :], pos_i[:, :]).then_inc(net_step, 1)
                e.wait_ge(net_step, POS)
                e.scalar_tensor_tensor(out=net, in0=w0_b, scalar=pos[:, :], in1=b0_b, op0=ALU.mult, op1=ALU.add)\
                    .then_inc(net_step, 1)
                net_norm(PRE1, ST1, MV1, VE1, RSTD1, CEN1, GAIN1, g_b[0])
                net_silu(EXP1, PLUS1, REC1, SILU1)
                e.wait_ge(net_step, MM1)
                e.tensor_tensor(net, bank_y[:, :], b1_b, ALU.add).then_inc(net_step, 1)
                net_norm(PRE2, ST2, MV2, VE2, RSTD2, CEN2, GAIN2, g_b[1])
                net_silu(EXP2, PLUS2, REC2, SILU2)
                e.wait_ge(net_step, MM2)
                e.memset(table_sb[:, P:2 * P], -BIG)
                e.tensor_scalar(table_sb[:, 0:P], bank_y[0:H, 0:P], b2_col[:, :], None, ALU.add).then_inc(net_step, 1)

            def x_stats(m):
                wait(e, x_loaded, m, by=16)
                e.bn_stats(moments[:, 0, :], x_in[:, :]).then_inc(x_moments, 1)

            def y_stats(m):
                wait(e, wo_half[1], m)
                e.bn_stats(moments[:, 1, :], bank_y[:, :]).then_inc(y_moments, 1)

            def means_variances(at):
                last = None
                for i, (d, stats) in enumerate(((3, x_moments), (-1, y_moments))):
                    if at(d) is not None:
                        wait(e, stats, at(d))
                        e.nop(nofuse=True)
                        last = e.bn_aggr(mean_var[:, i, :], moments[:, i, :])
                last.then_inc(mean_var_done, 1)
                e.wait_ge(mean_var_done, step_count(at))
                e.tensor_scalar(var_eps[:, :], mean_var[:, :, 1], EPS, None, ALU.add).then_inc(var_eps_done, 1)

            def ln_apply(m):
                wait(e, rstd_done, m)
                wait(e, xt_psum, m, -1)
                e.tensor_scalar(xn[:, :], x_in[:, :], mean_var[:, 0, 0:1], rstd[:, 0:1], ALU.subtract, ALU.mult)\
                    .then_inc(xn_ready, 1)

            def split_xt(m):
                wait(e, xt_h_ready, m)
                e.tensor_tensor(xt_l[:, :, :], bank_t[:, :].rearrange("p (c t) -> p c t", c=KC),
                                xt_h[:, :, :].bitcast(F32), ALU.subtract).then_inc(xt_ready, 1)

            def q_sums(m, p):
                if m[0] == 0:
                    return
                first, n = PARTS[p]
                n += p == 2
                wait_in_layer1(e, squares_ready[p], m)
                e.reduce_sum(ss[:, first:first + n], squares[:, 0:n * DH].rearrange("p (h d) -> p h d", h=n), AX.X)\
                    .then_inc(q_sum[p], 1)

            def q_scale_out(m, p):
                first, n = PARTS[p]
                bank = bank_q[p % 2]
                if m[0] == 1:
                    wait_in_layer1(e, q_norm[p], m)
                    wait(e, qt_psum[1], m, -1)
                    last = e.tensor_tensor(
                        q_nat[:, first * DH:(first + n) * DH].rearrange("p (h d) -> p h d", h=n),
                        bank[:, 0:n * DH].rearrange("p (h d) -> p h d", h=n),
                        rnorm[:, first:first + n].unsqueeze(2).broadcast_to([P, n, DH]), ALU.mult)
                    if p < 2:
                        last.then_inc(q_done[p], 1)
                if p < 2:
                    return
                k0, v0, s0 = n * DH, (n + 1) * DH, (n + 2) * DH
                k2 = bank[:, k0:v0].unsqueeze(1).broadcast_to([P, 2, DH])
                wait(e, kt_psum, m, -1)
                if m[0] == 0:
                    wait(e, q_copied, m)
                    e.tensor_scalar(k_nat[:, :, :], k2, DH ** -0.5, None, ALU.mult)
                    e.scalar_tensor_tensor(out=nns_next[:, :], in0=bank[:, s0:s0 + H], scalar=-1.0,
                                           in1=null_bias_sb[:, 0, :], op0=ALU.mult, op1=ALU.subtract)\
                        .then_inc(nns_next_ready, 1)
                else:
                    e.scalar_tensor_tensor(out=k_nat[:, :, :], in0=k2, scalar=rnorm[:, H:H + 1],
                                           in1=k_mul[:, :].unsqueeze(1).broadcast_to([P, 2, DH]),
                                           op0=ALU.mult, op1=ALU.mult)
                    e.tensor_tensor(null_s[:, :], bank[:, s0:s0 + H], rnorm[:, 0:H], ALU.mult)\
                        .then_inc(null_s_done, 1)
                    wait_in_layer1(e, null_s_done, m)
                    e.scalar_tensor_tensor(out=nns_next[:, :], in0=null_s[:, :], scalar=-1.0,
                                           in1=null_bias_sb[:, 1, :], op0=ALU.mult, op1=ALU.subtract)\
                        .then_inc(nns_next_ready, 1)
                wait(e, v_ready, m, -1)
                e.tensor_tensor(v_raw[:, :], bank[:, v0:s0], null_v[:, :], ALU.subtract).then_inc(q_done[2], 1)

            def split_qt(m, half):
                wait(e, qt_h_ready[half], m)
                e.tensor_tensor(qt_l[:, 4 * half:4 * half + 4, :], bank_t[:, :].rearrange("p (c t) -> p c t", c=4),
                                qt_h[:, 4 * half:4 * half + 4, :].bitcast(F32), ALU.subtract)\
                    .then_inc(qt_ready[half], 1)

            def split_kt(m):
                wait(e, kt_h_ready, m)
                for half in range(2):
                    r = slice(half * DH, (half + 1) * DH)
                    last = e.tensor_tensor(kt_l[r, half, :], bank_t[r, 0:P], kt_h[r, half, :].bitcast(F32), ALU.subtract)
                last.then_inc(kt_ready, 1)

            def split_v(m):
                wait(e, v_h_ready, m)
                h2 = v_h[:, :].rearrange("p (a b d) -> p a b d", a=2, b=2)
                l2 = v_l[:, :].rearrange("p (a b d) -> p a b d", a=2, b=2)
                for half in range(2):
                    last = e.tensor_tensor(l2[:, half, half, :], v_raw[:, :], h2[:, half, half, :].bitcast(F32),
                                           ALU.subtract)
                last.then_inc(v_ready, 1)

            def take_null_scores(m):
                wait(e, nns_next_ready, m)
                e.tensor_copy(nns[:, :], nns_next[:, :]).then_inc(nns_ready, 1)

            def take_mask(m):
                if opens_layer(m):
                    e.wait_ge(rows_loaded, 16 * ROW_LOADS)
                wait(e, bias_ready[3], m, -1)
                e.tensor_scalar(mask_row[:, :], mask[:, m[0], m[1], :], -1.0, BIG, ALU.add, ALU.mult)\
                    .then_inc(mask_ready, 1)

            def scores(m, g):
                hs = slice(HG * g, HG * (g + 1))
                wait(e, s_psum[g], m)
                wait(e, bias_ready[g], m)
                wait(e, exp_ready[(g + 2) % G], m, -1 if g < 2 else 0)
                if g == 0:
                    wait(e, nns_ready, m)
                e.tensor_scalar(s_sb[:, g % 2, :, P], nns[:, hs], -1.0, None, ALU.mult)
                for j in range(HG):
                    h = HG * g + j
                    last = e.tensor_tensor_reduce(s_sb[:, g % 2, j, 0:P], bank_s[g % 2][:, j * P:(j + 1) * P],
                                                  bias_g[:, g % 2, j, :], 1.0, LOWEST, ALU.add, ALU.max,
                                                  mx[:, h:h + 1])
                last.then_inc(s_ready[g], 1)
                wait(e, s_ready[g], m)
                e.scalar_tensor_tensor(out=neg_m[:, hs], in0=mx[:, hs], scalar=-1.0, in1=nns[:, hs],
                                       op0=ALU.mult, op1=ALU.min).then_inc(neg_m_ready[g], 1)

            def sums(m, g):
                hs = slice(HG * g, HG * (g + 1))
                wait(e, exp_ready[g], m)
                e.reciprocal(rden[:, hs], esum[:, hs]).then_inc(rden_ready[g], 1)

            def split_pt(m, g):
                wait(e, pt_h_ready[g], m)
                e.tensor_tensor(pt_l[:, g % 2, :, :], bank_p[:, :].rearrange("p (h i) -> p h i", h=HG),
                                pt_h[:, g % 2, :, :].bitcast(F32), ALU.subtract).then_inc(pt_ready[g], 1)

            def split_ot(m, half):
                cs = slice(4 * half, 4 * half + 4)
                wait(e, ot_h_ready[half], m)
                e.scalar_tensor_tensor(out=ot_l[:, cs, :], in0=bank_o[:, :].rearrange("p (c t) -> p c t", c=4),
                                       scalar=null_v_col[:, :], in1=ot_h[:, cs, :].bitcast(F32),
                                       op0=ALU.add, op1=ALU.subtract).then_inc(ot_ready[half], 1)

            def y_center(m):
                wait(e, mean_var_done, m, 4)
                e.scalar_tensor_tensor(out=y_t, in0=bank_y[:, :], scalar=mean_var[:, 1, 0:1], in1=g_out_sb[:, m[0], :],
                                       op0=ALU.subtract, op1=ALU.mult).then_inc(y_out_of_psum, 1)

            def y_finish(m):
                wait(e, rstd_done, m, 4)
                wait(e, y_out_of_psum, m)
                wait(e, res_loaded, m, by=16)
                wait(e, x_stored, m, -1, by=16)
                e.scalar_tensor_tensor(out=x_out, in0=y_t, scalar=rstd[:, 1:2], in1=x_res[:, :],
                                       op0=ALU.mult, op1=ALU.add).then_inc(x_out_ready, 1)

            def step(at):
                def on(d, stage, *which):
                    if at(d) is not None:
                        stage(at(d), *which)

                on(0, scores, 0)
                on(1, split_xt)
                on(2, ln_apply)
                on(0, scores, 1)
                on(0, sums, 0)
                on(0, scores, 2)
                on(1, take_mask)
                on(3, x_stats)
                on(1, q_sums, 0)
                on(-1, split_ot, 1)
                on(0, sums, 1)
                on(0, scores, 3)
                on(1, q_sums, 1)
                on(1, q_scale_out, 0)
                on(0, sums, 2)
                on(0, split_v)
                on(0, split_pt, 0)
                on(-1, y_stats)
                means_variances(at)
                on(-1, y_center)
                on(0, sums, 3)
                on(1, q_scale_out, 1)
                on(1, q_sums, 2)
                on(0, split_pt, 1)
                on(-1, y_finish)
                on(1, split_qt, 0)
                on(1, q_scale_out, 2)
                on(0, split_pt, 2)
                on(0, split_ot, 0)
                on(1, split_qt, 1)
                on(0, split_pt, 3)
                on(1, take_null_scores)
                on(1, split_kt)

            def between(n):
                if n == B - 2:
                    null_columns(1, w1_sb[:, 0:2, :].rearrange("p c n -> p (c n)"))
                if n == B - 1:
                    project_weights(1)
                if n in (B, B + 1):
                    output_weights(1, n - B)

            net_table()
            null_columns(0, y_out[:, :, :].rearrange("p a n -> p (a n)"))
            project_weights(0)
            output_weights(0, 0)
            output_weights(0, 1)
            stream(e, step, between)

        @block.tensor
        def _(e):
            e.wait_ge(consts_ready, 4)

            def product(out, passes):
                for k, (a, b) in enumerate(passes):
                    last = e.matmul(out, a, b, start=(k == 0), stop=(k == len(passes) - 1))
                return last

            def net_transposes(silu, tp):
                e.wait_ge(net_step, silu)
                for c in range(KC):
                    last = e.transpose(bank_t[:, c * P:(c + 1) * P], net[:, c * P:(c + 1) * P], ident[:, :])
                last.then_inc(net_step, 1)

            net_transposes(SILU1, TP1)
            e.wait_ge(net_step, TCOPY1)
            product(bank_y[:, :], [(net_t[:, c, :], w1_sb[:, c, :]) for c in range(KC)]).then_inc(net_step, 1)
            net_transposes(SILU2, TP2)
            e.wait_ge(net_step, TCOPY2)
            product(bank_y[0:H, 0:P], [(w2_sb[:, c, :], net_t[:, c, :]) for c in range(KC)]).then_inc(net_step, 1)

            def transpose_x(m):
                wait(e, xn_ready, m)
                if opens_layer(m) and m[0] == 0:
                    e.wait_ge(net_step, TABLE)
                else:
                    wait(e, kt_ready, m, -1)
                for c in range(KC):
                    last = e.transpose(bank_t[:, c * P:(c + 1) * P], xn[:, c * P:(c + 1) * P], ident[:, :])
                last.then_inc(xt_psum, 1)

            def project(m, p):
                lo, hi = part_columns(p)
                if opens_layer(m) and p == 0:
                    e.wait_ge(wq_ready, m[0] + 1)
                if p == 0:
                    wait(e, xt_ready, m)
                    wait(e, q_done[2], m, -1)
                elif p == 1:
                    wait(e, q_done[1], m, -1)
                else:
                    wait(e, q_done[0], m)
                passes = []
                for c in range(KC):
                    passes += [(xt_h[:, c, :], wq_h[:, c, lo:hi]), (xt_h[:, c, :], wq_l[:, c, lo:hi]),
                               (xt_l[:, c, :], wq_h[:, c, lo:hi])]
                product(bank_q[p % 2][:, 0:hi - lo], passes).then_inc(q_psum[p], 1)

            def transpose_q(m, half):
                if half == 0:
                    wait(e, q_done[0], m)
                    wait(e, q_done[1], m)
                    wait(e, xt_ready, m)
                else:
                    wait(e, q_done[2], m)
                    wait(e, qt_ready[0], m)
                for c in range(4):
                    k = 4 * half + c
                    last = e.transpose(bank_t[:, c * P:(c + 1) * P], q_nat[:, k * P:(k + 1) * P], ident[:, :])
                last.then_inc(qt_psum[half], 1)

            def transpose_k(m):
                wait(e, qt_ready[1], m)
                e.transpose(bank_t[:, 0:P], k_nat[:, :, :].rearrange("p a d -> p (a d)"), ident[:, :])\
                    .then_inc(kt_psum, 1)

            def scores(m, g):
                if g % 2 == 0:
                    wait(e, qt_ready[g // 2], m)
                if g == 0:
                    wait(e, kt_ready, m)
                wait(e, s_ready[(g + 2) % G], m, -1 if g < 2 else 0)
                kh, kl = (t[:, :, :].rearrange("p a j -> p (a j)") for t in (kt_h, kt_l))
                for j in range(2):
                    c = 2 * g + j
                    last = product(bank_s[g % 2][:, j * 2 * P:(j + 1) * 2 * P],
                                   [(qt_h[:, c, :], kh), (qt_h[:, c, :], kl), (qt_l[:, c, :], kh)])
                last.then_inc(s_psum[g], 1)

            def transpose_p(m, g):
                wait(e, p_ready[g], m)
                wait(e, pt_ready[(g + 3) % G], m, -1 if g == 0 else 0)
                for j in range(HG):
                    last = e.transpose(bank_p[:, j * P:(j + 1) * P], p_sb[:, g % 2, j, :], ident[:, :])
                last.then_inc(pt_psum[g], 1)

            def attend(m, g):
                wait(e, pt_ready[g], m)
                if g == 0:
                    wait(e, v_ready, m)
                if g % 2 == 0:
                    wait(e, ot_ready[1 - g // 2], m, -1 if g == 0 else 0)
                passes = []
                for odd in range(2):
                    vh, vl = (t[:, odd * P:(odd + 1) * P] for t in (v_h, v_l))
                    ph, pl = (t[:, g % 2, odd::2, :] for t in (pt_h, pt_l))
                    passes += [(vh, ph), (vl, ph), (vh, pl)]
                o = bank_o[:, (g % 2) * 2 * P:(g % 2 + 1) * 2 * P].rearrange("p (c i) -> p c i", c=2)
                product(o, passes).then_inc(pv_psum[g], 1)

            def output(m, c0, c1):
                if opens_layer(m) and c0 % 4 == 0:
                    e.wait_ge(wo_ready, 2 * m[0] + c0 // 4 + 1)
                if c0 == 0:
                    wait(e, y_out_of_psum, m, -1)
                if c0 % 4 == 0:
                    wait(e, ot_ready[c0 // 4], m)
                for c in range(c0, c1):
                    for k, (a, b) in enumerate(((ot_h, wo_h), (ot_h, wo_l), (ot_l, wo_h))):
                        last = e.matmul(bank_y[:, :], a[:, c, :], b[:, c, :], start=(c == 0 and k == 0),
                                        stop=(c == OC - 1 and k == 2))
                if c1 % 4 == 0:
                    last.then_inc(wo_half[c1 // 4 - 1], 1)

            def step(at):
                def on(d, stage, *which):
                    if at(d) is not None:
                        stage(at(d), *which)

                on(0, scores, 0)
                on(1, transpose_x)
                on(0, scores, 1)
                on(-1, attend, 2)
                on(0, scores, 2)
                on(1, project, 0)
                on(-1, attend, 3)
                on(1, project, 1)
                on(0, scores, 3)
                on(-1, output, 4, 6)
                on(0, transpose_p, 0)
                on(-1, output, 6, 8)
                on(1, project, 2)
                on(0, transpose_p, 1)
                on(0, attend, 0)
                on(1, transpose_q, 0)
                on(0, transpose_p, 2)
                on(0, attend, 1)
                on(1, transpose_q, 1)
                on(0, transpose_p, 3)
                on(0, output, 0, 2)
                on(1, transpose_k)
                on(0, output, 2, 4)

            stream(e, step)


_INS = ["x", "fside_16xSxS_0", "cond_64", "mask_BxS_bk0", "mask_BxS_bf1",
        "L0_cond_g_in", "L0_cond_null_attn_bias", "L0_cond_Wq", "L0_cond_Wkv", "L0_cond_Wo", "L0_cond_g_out",
        "L1_cond_g_norm", "L1_cond_Wq", "L1_cond_Wkv", "L1_cond_q_scale", "L1_cond_k_scale",
        "L1_cond_null_attn_bias", "L1_cond_w0", "L1_cond_b0", "L1_cond_g0", "L1_cond_w1", "L1_cond_b1",
        "L1_cond_g1", "L1_cond_w2", "L1_cond_b2", "L1_cond_Wout", "L1_cond_g_out"]


def kernel(**inputs):
    import numpy as _np
    import concourse.bacc as _bacc
    from concourse import mybir as _mybir
    from concourse.bass_utils import run_bass_kernel_spmd as _run

    nc = _bacc.Bacc("TRN2", target_bir_lowering=False, num_devices=1)
    arrays, a = {}, {}
    for name in _INS:
        v = _np.ascontiguousarray(inputs[name])
        arrays[f"in_{name}"] = v
        a[name] = nc.dram_tensor(f"in_{name}", v.shape, _mybir.dt.from_np(v.dtype), kind="ExternalInput").ap()
    out = nc.dram_tensor("out_x", (B, P, D), F32, kind="ExternalOutput").ap()
    build(nc, a["x"], a["fside_16xSxS_0"], a["cond_64"], a["mask_BxS_bk0"], a["mask_BxS_bf1"],
          [a["L0_cond_g_in"], a["L1_cond_g_norm"]],
          [a["L0_cond_null_attn_bias"], a["L1_cond_null_attn_bias"]],
          [a["L0_cond_Wq"], a["L1_cond_Wq"]], [a["L0_cond_Wkv"], a["L1_cond_Wkv"]],
          [a["L0_cond_Wo"], a["L1_cond_Wout"]], [a["L0_cond_g_out"], a["L1_cond_g_out"]],
          a["L1_cond_q_scale"], a["L1_cond_k_scale"], a["L1_cond_w0"], a["L1_cond_b0"], a["L1_cond_g0"],
          a["L1_cond_w1"], a["L1_cond_b1"], a["L1_cond_g1"], a["L1_cond_w2"], a["L1_cond_b2"], out)
    r = _run(nc, [arrays], core_ids=[0])
    return r.results[0]["out_x"]
```

```python
from contextlib import ExitStack

import concourse.bass as bass
from concourse import mybir

ALU = mybir.AluOpType
ACT = mybir.ActivationFunctionType
AX = mybir.AxisListType
F32 = mybir.dt.float32
F32R = mybir.dt.float32r
I32 = mybir.dt.int32
U8 = mybir.dt.uint8

P = 128
B = 32
D = 512
H = 16
DH = 64
INNER = H * DH
LAYERS = 2
N = LAYERS * B
KC = D // P
OC = INNER // P
QKV = INNER + 2 * DH
W = QKV + H
G = 4
HG = H // G
PARTS = [(0, 6), (6, 6), (12, 4)]
EPS = 1e-5
TINY = 1e-24
BIG = 1e38
LOWEST = -3.4e38
FIRST, LAST = 3, B - 4
NULL_STEPS = [1, 2, B - 3, B - 2]


def part_columns(p):
    first, count = PARTS[p]
    return first * DH, (W if p == len(PARTS) - 1 else (first + count) * DH)


def count(m, d=0):
    layer, b = m
    return b + (layer * B + 1 + d)


def wait(e, sem, m, d=0, by=1):
    value = count(m, d) * by
    if not (isinstance(value, int) and value <= 0):
        e.wait_ge(sem, value)


def wait_in_layer1(e, sem, m, d=0):
    value = m[1] + (1 + d)
    if not (isinstance(value, int) and value <= 0):
        e.wait_ge(sem, value)


def step_count(at):
    return count(at(3)) if at(3) is not None else count(at(-1), 4)


def is_item(m, layer, b):
    return isinstance(m[1], int) and m == (layer, b)


def opens_layer(m):
    return is_item(m, m[0], 0)


def stream(e, step, between=None):
    def straight(first, last):
        for n in range(first, last):
            if between:
                between(n)
            step(lambda d, n=n: ((n + d) // B, (n + d) % B) if 0 <= n + d < N else None)

    straight(-3, FIRST)
    for layer in range(LAYERS):
        with e.Fori(FIRST, LAST + 1) as i:
            step(lambda d: (layer, i + d))
        straight(layer * B + LAST + 1, (layer + 1) * B + FIRST if layer + 1 < LAYERS else N + 1)


def build(nc, x, bias0, cond, mask0, mask1, g_in, null_bias, wq, wkv, wo, g_out, q_scale, k_scale,
          w0, b0, g0, w1, b1, g1, w2, b2, out):
    x_mid = nc.dram_tensor("x_mid", (B, P, D), F32, kind="Internal").ap()
    table = nc.dram_tensor("bias_table", (H, P, 2 * P), F32, kind="Internal").ap()
    x_of = [x, x_mid]
    out_of = [x_mid, out]

    with ExitStack() as ctx:
        def sb(name, shape, dt=F32):
            return ctx.enter_context(nc.sbuf_tensor(name, shape, dt))

        def psum(name):
            return ctx.enter_context(nc.psum_tensor(name, [P, 512], F32))

        def sem(name):
            return ctx.enter_context(nc.semaphore(name))

        def sems(name, n):
            return [sem(f"{name}{i}") for i in range(n)]

        wq_h = sb("wq_h", [P, KC, W], F32R)
        wq_l = sb("wq_l", [P, KC, W], F32R)
        wo_h = sb("wo_h", [P, OC, D], F32R)
        wo_l = sb("wo_l", [P, OC, D], F32R)
        wq_raw = sb("wq_raw", [P, KC, QKV])
        wo_raw = sb("wo_raw", [P, OC, D])
        w_null = sb("w_null", [P, KC, H])
        bias = sb("bias", [P, LAYERS, H, P])
        mask = sb("mask", [P, LAYERS, B, P], U8)
        g_in_sb = sb("g_in_sb", [P, LAYERS, KC])
        g_out_sb = sb("g_out_sb", [P, LAYERS, D])
        null_bias_sb = sb("null_bias_sb", [P, LAYERS, H])
        null_k = sb("null_k", [P, DH])
        null_kn = sb("null_kn", [P, LAYERS, DH])
        null_v = sb("null_v", [P, DH])
        null_v_col = sb("null_v_col", [P, 1])
        qs = sb("qs", [P, DH])
        k_mul = sb("k_mul", [P, DH])
        nk_sq = sb("nk_sq", [P, DH])
        nk_ss = sb("nk_ss", [P, 2])
        ident = sb("ident", [P, P])
        minus_half = sb("minus_half", [P, 8])
        x_in = sb("x_in", [P, D])
        x_res = sb("x_res", [P, D])
        xn = sb("xn", [P, D])
        xt_h = sb("xt_h", [P, KC, P], F32R)
        xt_l = sb("xt_l", [P, KC, P], F32R)
        q_nat = sb("q_nat", [P, INNER])
        squares = sb("squares", [P, 6 * DH])
        k_nat = sb("k_nat", [P, 2, DH])
        v_raw = sb("v_raw", [P, DH])
        moments = sb("moments", [P, 2, 6])
        mean_var = sb("mean_var", [P, 2, 2])
        var_eps = sb("var_eps", [P, 2])
        rstd = sb("rstd", [P, 2])
        ss = sb("ss", [P, H + 1])
        ssc = sb("ssc", [P, H + 1])
        rnorm = sb("rnorm", [P, H + 1])
        null_s = sb("null_s", [P, H])
        nns_next = sb("nns_next", [P, H])
        nns = sb("nns", [P, H])
        qt_h = sb("qt_h", [P, OC, P], F32R)
        qt_l = sb("qt_l", [P, OC, P], F32R)
        kt_h = sb("kt_h", [P, 2, P], F32R)
        kt_l = sb("kt_l", [P, 2, P], F32R)
        v_h = sb("v_h", [P, 2 * P], F32R)
        v_l = sb("v_l", [P, 2 * P], F32R)
        mask_row = sb("mask_row", [P, P])
        bias_g = sb("bias_g", [P, 2, HG, P])
        s_sb = sb("s_sb", [P, 2, HG, P + 1])
        mx = sb("mx", [P, H])
        neg_m = sb("neg_m", [P, H])
        esum = sb("esum", [P, H])
        rden = sb("rden", [P, H])
        p_raw = sb("p_raw", [P, 2, HG, P + 1])
        p_sb = sb("p_sb", [P, 2, HG, P])
        pt_h = sb("pt_h", [P, 2, HG, P], F32R)
        pt_l = sb("pt_l", [P, 2, HG, P], F32R)
        ot_h = sb("ot_h", [P, OC, P], F32R)
        ot_l = sb("ot_l", [P, OC, P], F32R)
        y_out = sb("y_out", [P, 2, D])
        y_t, x_out = y_out[:, 0, :], y_out[:, 1, :]
        w1_sb = sb("w1_sb", [P, KC, D])
        w2_sb = sb("w2_sb", [P, KC, H])
        b2_col = sb("b2_col", [H, 1])
        pos_i = sb("pos_i", [P, 1], I32)
        pos = sb("pos", [P, 1])
        table_sb = squares[0:H, 0:2 * P]
        flat = lambda t: t[:, :, :, :].rearrange("p a h j -> p a (h j)")
        w0_b, b0_b = flat(p_raw)[:, 0, 0:D], flat(p_raw)[:, 1, 0:D]
        g_b, b1_b = [flat(p_sb)[:, 0, :], flat(p_sb)[:, 1, :]], flat(s_sb)[:, 0, 0:D]
        net = y_out[:, 0, :]
        net_t = y_out[:, 1, :].rearrange("p (c t) -> p c t", c=KC)
        net_e = x_res[:, :]
        wide = lambda t: t.rearrange("p a n -> p (a n)")
        null_scratch = [[wide(bias[:, 1, 0:8, :]), wide(bias[:, 1, 8:16, :]),
                         bias_g[:, :, :, :].rearrange("p a h j -> p (a h j)"), q_nat[:, :]],
                        [wide(w1_sb[:, 0:2, :]), wide(w1_sb[:, 2:4, :])] * 2]

        bank_s = [psum("bank_s0"), psum("bank_s1")]
        bank_p = psum("bank_p")
        bank_q = [psum("bank_q0"), psum("bank_q1")]
        bank_o = psum("bank_o")
        bank_t = psum("bank_t")
        bank_y = psum("bank_y")

        wq_loaded = sems("wq_loaded", 3)
        wo_loaded = sem("wo_loaded")
        small_loaded = sem("small_loaded")
        rows_loaded = sem("rows_loaded")
        bias0_loaded = sem("bias0_loaded")
        net_loaded = sem("net_loaded")
        table_stored = sem("table_stored")
        bias1_loaded = sem("bias1_loaded")
        consts_ready = sem("consts_ready")
        zeros_ready = sem("zeros_ready")
        causal_ready = sem("causal_ready")
        nk_step = sem("nk_step")
        null_prod = sem("null_prod")
        null_ready = sem("null_ready")
        wq_h_ready = sems("wq_h_ready", 3)
        wn_h_ready = sem("wn_h_ready")
        wq_ready = sems("wq_ready", 3)
        wo_h_ready = sem("wo_h_ready")
        wo_ready = sem("wo_ready")
        net_step = sem("net_step")
        x_loaded = sem("x_loaded")
        res_loaded = sem("res_loaded")
        x_stored = sem("x_stored")
        x_moments = sem("x_moments")
        y_moments = sem("y_moments")
        mean_var_done = sem("mean_var_done")
        var_eps_done = sem("var_eps_done")
        rstd_done = sem("rstd_done")
        xn_ready = sem("xn_ready")
        xt_psum = sem("xt_psum")
        xt_h_ready = sem("xt_h_ready")
        xt_ready = sem("xt_ready")
        q_psum = sems("q_psum", 3)
        q_copied = sem("q_copied")
        squares_ready = sems("squares_ready", 3)
        q_sum = sems("q_sum", 3)
        q_clamp = sems("q_clamp", 3)
        q_norm = sems("q_norm", 3)
        q_done = sems("q_done", 3)
        null_s_done = sem("null_s_done")
        nns_next_ready = sem("nns_next_ready")
        nns_ready = sem("nns_ready")
        qt_psum = sems("qt_psum", 2)
        qt_h_ready = sems("qt_h_ready", 2)
        qt_ready = sems("qt_ready", 2)
        kt_psum = sem("kt_psum")
        kt_h_ready = sem("kt_h_ready")
        kt_ready = sem("kt_ready")
        v_h_ready = sem("v_h_ready")
        v_ready = sem("v_ready")
        mask_ready = sem("mask_ready")
        bias_ready = sems("bias_ready", G)
        s_psum = sems("s_psum", G)
        s_ready = sems("s_ready", G)
        neg_m_ready = sems("neg_m_ready", G)
        exp_ready = sems("exp_ready", G)
        rden_ready = sems("rden_ready", G)
        p_ready = sems("p_ready", G)
        pt_psum = sems("pt_psum", G)
        pt_h_ready = sems("pt_h_ready", G)
        pt_ready = sems("pt_ready", G)
        pv_psum = sems("pv_psum", G)
        ot_h_ready = sems("ot_h_ready", 2)
        ot_ready = sems("ot_ready", 2)
        wo_half = sems("wo_half", 2)
        y_out_of_psum = sem("y_out_of_psum")
        x_out_ready = sem("x_out_ready")

        WQ_LOADS = [1, 1, 2]
        SMALL_LOADS = 6 + 2 * LAYERS
        ROW_LOADS = 2 * LAYERS
        NET_LOADS = 8
        (POS, PRE1, ST1, MV1, VE1, RSTD1, CEN1, GAIN1, EXP1, PLUS1, REC1, SILU1, TP1, TCOPY1,
         MM1, PRE2, ST2, MV2, VE2, RSTD2, CEN2, GAIN2, EXP2, PLUS2, REC2, SILU2, TP2, TCOPY2,
         MM2, TABLE) = range(1, 31)

        block = ctx.enter_context(nc.Block())

        @block.sync
        def _(e):
            def load_wq(layer):
                for p, (first, n) in enumerate(PARTS):
                    cols = slice(first * DH, (first + n) * DH)
                    e.dma_start(wq_raw[:, :, cols], wq[layer][:, cols].rearrange("(c p) n -> p c n", p=P))\
                        .then_inc(wq_loaded[p], 16)
                e.dma_start(wq_raw[:, :, INNER:QKV], wkv[layer].rearrange("(c p) n -> p c n", p=P))\
                    .then_inc(wq_loaded[2], 16)

            def load_wo(layer):
                e.dma_start(wo_raw[:, :, :], wo[layer].rearrange("(c p) n -> p c n", p=P)).then_inc(wo_loaded, 16)

            def row(v):
                return v.rearrange("(a n) -> a n", a=1)

            def small(dst, src, **how):
                e.dma_start(dst, src, **how).then_inc(small_loaded, 16)

            small(null_k[:, :], cond[0:1, :].broadcast_to([P, DH]))
            small(qs[:, :], row(q_scale).broadcast_to([P, DH]))
            small(k_mul[:, :], row(k_scale).broadcast_to([P, DH]))
            small(null_v[:, :], cond[1:2, :].broadcast_to([P, DH]))
            for half in range(2):
                small(null_v_col[half * DH:(half + 1) * DH, :], cond[1:2, :].rearrange("a d -> d a"))
            for layer in range(LAYERS):
                small(g_in_sb[:, layer, :], g_in[layer].rearrange("(c p) -> p c", p=P), allow_slow_non_contiguous=True)
                small(null_bias_sb[:, layer, :], row(null_bias[layer]).broadcast_to([P, H]))
            def step(at):
                if (m := at(-1)) is not None:
                    if is_item(m, 0, 0):
                        e.wait_ge(net_step, TABLE)
                    wait(e, x_out_ready, m, -1)
                    e.dma_start(x_res[:, :], x_of[m[0]][m[1]]).then_inc(res_loaded, 16)
                if (m := at(3)) is not None:
                    wait(e, xn_ready, m, -1)
                    if m[0] == 1:
                        e.wait_ge(x_stored, (m[1] + 1) * 16)
                    e.dma_start(x_in[:, :], x_of[m[0]][m[1]]).then_inc(x_loaded, 16)
                if (m := at(-1)) is not None:
                    wait(e, x_out_ready, m)
                    e.dma_start(out_of[m[0]][m[1]], x_out).then_inc(x_stored, 16)

            def between(n):
                if n == -2:
                    load_wq(0)
                if n == -1:
                    load_wo(0)
                    e.dma_start(bias[:, 0, :, :], bias0.rearrange("h i j -> i h j")).then_inc(bias0_loaded, 16)
                    for layer in range(LAYERS):
                        e.dma_start(g_out_sb[:, layer, :], row(g_out[layer]).broadcast_to([P, D])).then_inc(rows_loaded, 16)
                        m = (mask0, mask1)[layer].rearrange("(a b) s -> a b s", a=1)
                        e.dma_start(mask[:, layer, :, :], m.broadcast_to([P, B, P])).then_inc(rows_loaded, 16)
                if n == 0:
                    for p in range(3):
                        e.wait_ge(wq_ready[p], 1)
                    load_wq(1)
                if n == 1:
                    e.wait_ge(wo_ready, 2)
                    load_wo(1)
                    e.wait_ge(net_step, TABLE)
                    e.dma_start(table, table_sb.unsqueeze(1).broadcast_to([H, P, 2 * P])).then_inc(table_stored, 16)
                if n == 2:
                    e.wait_ge(table_stored, 16)
                    shifted = bass.AP(table.tensor, P - 1, [[2 * P - 1, P], [2 * P * P, H], [1, P]])
                    e.dma_start(bias[:, 1, :, :], shifted).then_inc(bias1_loaded, 16)

            stream(e, step, between)
            e.wait_ge(x_stored, 16 * N)

        @block.gpsimd
        def _(e):
            e.memset(ident[:, :], 0.0).then_inc(consts_ready, 1)
            e.memset(minus_half[:, :], -0.5).then_inc(consts_ready, 1)
            e.iota(pos_i[:, :], pattern=[[0, 1]], base=P - 1, channel_multiplier=-1).then_inc(consts_ready, 1)
            e.wait_ge(consts_ready, 3)
            e.affine_select(out=ident[:, :], in_=ident[:, :], compare_op=ALU.not_equal, fill=1.0, base=0,
                            pattern=[[-1, P]], channel_multiplier=1).then_inc(consts_ready, 1)
            e.wait_ge(nk_step, 4)
            e.tensor_tensor(nk_ss[:, 1:2], nk_ss[:, 0:1], minus_half[:, 0:1], ALU.pow).then_inc(nk_step, 1)

            def net_deviation(ve):
                e.wait_ge(net_step, ve)
                e.tensor_tensor(rstd[:, 0:1], var_eps[:, 0:1], minus_half[:, 0:1], ALU.pow).then_inc(net_step, 1)

            net_deviation(VE1)

            def null_product(layer, c):
                k = KC * layer + c
                if c == 0:
                    for p in range(3):
                        e.wait_ge(wq_loaded[p], 16 * WQ_LOADS[p] * (layer + 1))
                    e.wait_ge(nk_step, 6)
                if layer and c >= 2:
                    e.wait_ge(null_ready, k - 1)
                e.tensor_tensor(null_scratch[layer][c].rearrange("p (h d) -> p h d", h=H),
                                wq_raw[:, c, 0:INNER].rearrange("p (h d) -> p h d", h=H),
                                null_kn[:, layer, :].unsqueeze(1).broadcast_to([P, H, DH]), ALU.mult)\
                    .then_inc(null_prod, 1)

            def between(n):
                if n == -2:
                    for c in range(KC):
                        null_product(0, c)
                if n == -1:
                    for c in range(OC):
                        e.wait_ge(wo_h_ready, c + 1)
                        last = e.tensor_tensor(wo_l[:, c, :], wo_raw[:, c, :], wo_h[:, c, :].bitcast(F32), ALU.subtract)
                    last.then_inc(wo_ready, 2)
                    net_deviation(VE2)
                    e.wait_ge(bias0_loaded, 16)
                    e.affine_select(out=bias[:, 0, :, :], in_=bias[:, 0, :, :], compare_op=ALU.is_ge, fill=-BIG,
                                    base=0, pattern=[[0, H], [-1, P]], channel_multiplier=1).then_inc(causal_ready, 1)
                if n in NULL_STEPS:
                    null_product(1, NULL_STEPS.index(n))

            def masked_bias(m, g):
                if opens_layer(m):
                    if m[0] == 0:
                        e.wait_ge(causal_ready, 1)
                    else:
                        e.wait_ge(bias1_loaded, 16)
                if g < 2:
                    wait(e, mask_ready, m)
                wait(e, s_ready[(g + 2) % G], m, -1 if g < 2 else 0)
                e.tensor_tensor(bias_g[:, g % 2, :, :], bias[:, m[0], HG * g:HG * (g + 1), :],
                                mask_row[:, :].unsqueeze(1).broadcast_to([P, HG, P]), ALU.add)\
                    .then_inc(bias_ready[g], 1)

            def normalise(m, g):
                wait(e, rden_ready[g], m)
                wait(e, pt_psum[(g + 2) % G], m, -1 if g < 2 else 0)
                r = rden[:, HG * g:HG * (g + 1)].unsqueeze(2).broadcast_to([P, HG, P])
                e.tensor_tensor(p_sb[:, g % 2, :, :], p_raw[:, g % 2, :, 0:P], r, ALU.mult).then_inc(p_ready[g], 1)

            def norms(m, p):
                if m[0] == 0:
                    return
                first, n = PARTS[p]
                n += p == 2
                wait_in_layer1(e, q_sum[p], m)
                e.nop(nofuse=True)
                e.tensor_scalar(ssc[:, first:first + n], ss[:, first:first + n], TINY, None, ALU.max)\
                    .then_inc(q_clamp[p], 1)
                wait_in_layer1(e, q_clamp[p], m)
                e.tensor_tensor(rnorm[:, first:first + n], ssc[:, first:first + n], minus_half[:, 0:n], ALU.pow)\
                    .then_inc(q_norm[p], 1)

            def inverse_deviations(at):
                e.wait_ge(var_eps_done, step_count(at))
                e.tensor_tensor(rstd[:, :], var_eps[:, :], minus_half[:, 0:2], ALU.pow).then_inc(rstd_done, 1)

            def step(at):
                def on(d, stage, *which):
                    if at(d) is not None:
                        stage(at(d), *which)

                on(0, masked_bias, 2)
                on(0, normalise, 0)
                on(1, norms, 0)
                on(0, masked_bias, 3)
                on(1, norms, 1)
                on(0, normalise, 1)
                on(1, norms, 2)
                on(0, normalise, 2)
                on(1, masked_bias, 0)
                on(0, normalise, 3)
                on(1, masked_bias, 1)
                inverse_deviations(at)
            stream(e, step, between)

        @block.scalar
        def _(e):
            def net_load(dst, src):
                e.dma_start(dst, src).then_inc(net_loaded, 16)

            def row(v):
                return v.rearrange("(a n) -> a n", a=1).broadcast_to([P, D])

            net_load(w0_b, w0.broadcast_to([P, D]))
            net_load(b0_b, row(b0))
            net_load(g_b[0], row(g0))
            net_load(g_b[1], row(g1))
            net_load(b1_b, row(b1))
            net_load(w1_sb[:, :, :], w1.rearrange("(c p) n -> p c n", p=P))
            net_load(w2_sb[:, :, :], w2.rearrange("(c p) n -> p c n", p=P))
            net_load(b2_col[:, :], b2.rearrange("(h a) -> h a", a=1))

            def net_silu(gain, exp):
                e.wait_ge(net_step, gain)
                e.activation(net_e, net, ACT.Exp, scale=-1.0).then_inc(net_step, 1)

            def net_copy(tp, copy):
                e.wait_ge(net_step, tp)
                e.activation(net_t, bank_t[:, :].rearrange("p (c t) -> p c t", c=KC), ACT.Copy).then_inc(net_step, 1)

            def project_weights(layer, p):
                first, n = PARTS[p]
                lo, hi = first * DH, QKV if p == 2 else (first + n) * DH
                e.wait_ge(wq_loaded[p], 16 * WQ_LOADS[p] * (layer + 1))
                e.wait_ge(small_loaded, 16 * SMALL_LOADS)
                if layer:
                    e.wait_ge(q_psum[p], B)
                for c in range(KC):
                    e.activation(wq_h[:, c, lo:hi], wq_raw[:, c, lo:hi], ACT.Copy, scale=g_in_sb[:, layer, c:c + 1])\
                        .then_inc(wq_h_ready[p], 1)
                if p == 2 and layer == 0:
                    output_weights(0, 0)
                    output_weights(0, 1)
                if p == 2:
                    e.wait_ge(null_ready, KC * (layer + 1))
                    for c in range(KC):
                        e.activation(wq_h[:, c, QKV:W], w_null[:, c, :], ACT.Copy, scale=g_in_sb[:, layer, c:c + 1])\
                            .then_inc(wn_h_ready, 1)

            def output_weights(layer, half):
                e.wait_ge(wo_loaded, 16 * (layer + 1))
                if layer:
                    e.wait_ge(wo_half[half], B)
                for c in range(4 * half, 4 * half + 4):
                    e.activation(wo_h[:, c, :], wo_raw[:, c, :], ACT.Copy).then_inc(wo_h_ready, 1)

            def split_xt(m):
                wait(e, xt_psum, m)
                wait(e, q_psum[2], m, -1)
                e.activation(xt_h[:, :, :], bank_t[:, :].rearrange("p (c t) -> p c t", c=KC), ACT.Copy)\
                    .then_inc(xt_h_ready, 1)

            def q_out(m, p):
                first, n = PARTS[p]
                wait(e, q_psum[p], m)
                if m[0] == 0:
                    wait(e, qt_psum[1], m, -1)
                    e.activation(q_nat[:, first * DH:(first + n) * DH], bank_q[p % 2][:, 0:n * DH], ACT.Copy)\
                        .then_inc(q_done[p] if p < 2 else q_copied, 1)
                else:
                    n += p == 2
                    wait_in_layer1(e, q_sum[(p + 2) % 3], m, 0 if p else -1)
                    e.activation(squares[:, 0:n * DH], bank_q[p % 2][:, 0:n * DH], ACT.Square)\
                        .then_inc(squares_ready[p], 1)

            def split_qt(m, half):
                wait(e, qt_psum[half], m)
                wait(e, s_psum[2 * half + 1], m, -1)
                e.activation(qt_h[:, 4 * half:4 * half + 4, :], bank_t[:, :].rearrange("p (c t) -> p c t", c=4),
                             ACT.Copy).then_inc(qt_h_ready[half], 1)

            def split_kt(m):
                wait(e, kt_psum, m)
                wait(e, s_psum[3], m, -1)
                for half in range(2):
                    r = slice(half * DH, (half + 1) * DH)
                    last = e.activation(kt_h[r, half, :], bank_t[r, 0:P], ACT.Copy)
                last.then_inc(kt_h_ready, 1)

            def split_v(m):
                wait(e, q_done[2], m)
                wait(e, pv_psum[3], m, -1)
                v2 = v_h[:, 0:2 * P].rearrange("p (a b d) -> p a b d", a=2, b=2)
                for half in range(2):
                    last = e.activation(v2[:, half, half, :], v_raw[:, :], ACT.Copy)
                last.then_inc(v_h_ready, 1)

            def exps(m, g):
                wait(e, neg_m_ready[g], m)
                wait(e, p_ready[(g + 2) % G], m, -1 if g < 2 else 0)
                for j in range(HG):
                    h = HG * g + j
                    last = e.activation(p_raw[:, g % 2, j, :], s_sb[:, g % 2, j, :], ACT.Exp, bias=neg_m[:, h:h + 1],
                                        accum_out=esum[:, h:h + 1])
                last.then_inc(exp_ready[g], 1)

            def split_pt(m, g):
                wait(e, pt_psum[g], m)
                wait(e, pv_psum[(g + 2) % G], m, -1 if g < 2 else 0)
                e.activation(pt_h[:, g % 2, :, :], bank_p[:, :].rearrange("p (h i) -> p h i", h=HG), ACT.Copy)\
                    .then_inc(pt_h_ready[g], 1)

            def split_ot(m, half):
                wait(e, pv_psum[2 * half + 1], m)
                wait(e, wo_half[half], m, -1)
                e.activation(ot_h[:, 4 * half:4 * half + 4, :], bank_o[:, :].rearrange("p (c t) -> p c t", c=4),
                             ACT.Identity, bias=null_v_col[:, :]).then_inc(ot_h_ready[half], 1)

            def step(at):
                def on(d, stage, *which):
                    if at(d) is not None:
                        stage(at(d), *which)

                on(1, split_xt)
                on(1, start_weights)
                on(0, exps, 0)
                on(1, q_out, 0)
                on(1, next_weights, 0)
                on(0, exps, 1)
                on(1, q_out, 1)
                on(1, next_weights, 1)
                on(0, exps, 2)
                on(0, split_v)
                on(0, split_pt, 0)
                on(-1, split_ot, 1)
                on(1, q_out, 2)
                on(1, next_weights, 2)
                on(0, start_copy)
                on(1, split_qt, 0)
                on(1, start_exp)
                on(0, exps, 3)
                on(0, split_pt, 1)
                on(-1, next_output, 0)
                on(1, split_qt, 1)
                on(0, split_pt, 2)
                on(1, split_kt)
                on(0, split_ot, 0)
                on(0, split_pt, 3)
                on(-1, next_output, 1)

            def start_weights(m):
                if is_item(m, 0, 0):
                    project_weights(0, 2)

            def start_exp(m):
                if is_item(m, 0, 0):
                    net_silu(GAIN2, EXP2)

            def start_copy(m):
                if is_item(m, 0, 0):
                    net_copy(TP2, TCOPY2)

            def next_output(m, half):
                if is_item(m, 0, B - 1):
                    output_weights(1, half)

            def next_weights(m, p):
                if is_item(m, 0, B - 1):
                    project_weights(1, p)

            net_silu(GAIN1, EXP1)
            project_weights(0, 0)
            net_copy(TP1, TCOPY1)
            project_weights(0, 1)
            stream(e, step)

        @block.vector
        def _(e):
            for t in (kt_h, kt_l):
                e.memset(t[:, :, :].bitcast(F32), 0.0)
            e.memset(mean_var[:, :, :], 0.0)
            e.memset(v_h[:, :].bitcast(F32), 0.0)
            e.memset(v_l[:, :].bitcast(F32), 0.0).then_inc(zeros_ready, 1)
            e.wait_ge(zeros_ready, 1)

            e.wait_ge(small_loaded, 16 * SMALL_LOADS)
            e.tensor_scalar(null_kn[:, 0, :], null_k[:, :], DH ** -0.5, None, ALU.mult)
            e.tensor_tensor(nk_sq[:, :], null_k[:, :], null_k[:, :], ALU.mult).then_inc(nk_step, 1)
            e.scalar_tensor_tensor(out=k_mul[:, :], in0=k_mul[:, :], scalar=8.0, in1=qs[:, :], op0=ALU.mult,
                                   op1=ALU.mult).then_inc(nk_step, 1)
            e.wait_ge(nk_step, 2)
            e.reduce_sum(nk_ss[:, 1:2], nk_sq[:, :], AX.X).then_inc(nk_step, 1)
            e.wait_ge(nk_step, 3)
            e.tensor_scalar(nk_ss[:, 0:1], nk_ss[:, 1:2], TINY, None, ALU.max).then_inc(nk_step, 1)
            e.wait_ge(consts_ready, 4)
            e.wait_ge(nk_step, 5)
            e.scalar_tensor_tensor(out=null_kn[:, 1, :], in0=null_k[:, :], scalar=nk_ss[:, 1:2], in1=k_mul[:, :],
                                   op0=ALU.mult, op1=ALU.mult).then_inc(nk_step, 1)

            def null_sum(layer, c):
                k = KC * layer + c
                e.wait_ge(null_prod, k + 1)
                if layer:
                    e.wait_ge(wn_h_ready, KC)
                e.reduce_sum(w_null[:, c, :], null_scratch[layer][c].rearrange("p (h d) -> p h d", h=H), AX.X)\
                    .then_inc(null_ready, 1)

            def project_weights(layer, p):
                first, n = PARTS[p]
                lo, hi = first * DH, QKV if p == 2 else (first + n) * DH
                if layer:
                    e.wait_ge(q_psum[p], B)
                for c in range(KC):
                    e.wait_ge(wq_h_ready[p], KC * layer + c + 1)
                    last = e.scalar_tensor_tensor(out=wq_l[:, c, lo:hi], in0=wq_raw[:, c, lo:hi],
                                                  scalar=g_in_sb[:, layer, c:c + 1],
                                                  in1=wq_h[:, c, lo:hi].bitcast(F32),
                                                  op0=ALU.mult, op1=ALU.subtract)
                if p == 2:
                    if layer == 0:
                        null_sum(0, KC - 1)
                    for c in range(KC):
                        e.wait_ge(wn_h_ready, KC * layer + c + 1)
                        last = e.scalar_tensor_tensor(out=wq_l[:, c, QKV:W], in0=w_null[:, c, :],
                                                      scalar=g_in_sb[:, layer, c:c + 1],
                                                      in1=wq_h[:, c, QKV:W].bitcast(F32),
                                                      op0=ALU.mult, op1=ALU.subtract)
                last.then_inc(wq_ready[p], 1)

            def output_weights(layer, half):
                for c in range(4 * half, 4 * half + 4):
                    e.wait_ge(wo_h_ready, OC * layer + c + 1)
                    last = e.tensor_tensor(wo_l[:, c, :], wo_raw[:, c, :], wo_h[:, c, :].bitcast(F32), ALU.subtract)
                last.then_inc(wo_ready, 1)

            def net_norm(pre, st, mv, ve, rstd_step, cen, gain, g):
                e.wait_ge(net_step, pre)
                e.bn_stats(moments[:, 0, :], net).then_inc(net_step, 1)
                e.wait_ge(net_step, st)
                e.bn_aggr(mean_var[:, 0, :], moments[:, 0, :]).then_inc(net_step, 1)
                e.wait_ge(net_step, mv)
                e.tensor_scalar(var_eps[:, 0:1], mean_var[:, 0, 1:2], EPS, None, ALU.add).then_inc(net_step, 1)
                e.wait_ge(net_step, rstd_step)
                e.tensor_scalar(net, net, mean_var[:, 0, 0:1], rstd[:, 0:1], ALU.subtract, ALU.mult)\
                    .then_inc(net_step, 1)
                e.wait_ge(net_step, cen)
                e.tensor_tensor(net, net, g, ALU.mult).then_inc(net_step, 1)

            def net_silu(exp, plus, rec, quarters=range(4)):
                if 0 in quarters:
                    e.wait_ge(net_step, exp)
                    e.tensor_scalar(net_e, net_e, 1.0, None, ALU.add).then_inc(net_step, 1)
                    e.wait_ge(net_step, plus)
                for k in quarters:
                    part = net_e[:, k * P:(k + 1) * P]
                    last = e.reciprocal(part, part)
                if 3 in quarters:
                    last.then_inc(net_step, 1)
                    e.wait_ge(net_step, rec)
                    e.tensor_tensor(net, net, net_e, ALU.mult).then_inc(net_step, 1)

            def net_first_layer():
                e.wait_ge(net_loaded, 16 * NET_LOADS)
                e.wait_ge(consts_ready, 4)
                e.tensor_copy(pos[:, :], pos_i[:, :]).then_inc(net_step, 1)
                e.wait_ge(net_step, POS)
                e.scalar_tensor_tensor(out=net, in0=w0_b, scalar=pos[:, :], in1=b0_b, op0=ALU.mult, op1=ALU.add)\
                    .then_inc(net_step, 1)
                net_norm(PRE1, ST1, MV1, VE1, RSTD1, CEN1, GAIN1, g_b[0])
                net_silu(EXP1, PLUS1, REC1)

            def net_second_layer():
                e.wait_ge(net_step, MM1)
                e.tensor_tensor(net, bank_y[:, :], b1_b, ALU.add).then_inc(net_step, 1)
                net_norm(PRE2, ST2, MV2, VE2, RSTD2, CEN2, GAIN2, g_b[1])

            def net_table():
                e.wait_ge(net_step, MM2)
                e.memset(table_sb[:, P:2 * P], -BIG)
                e.tensor_scalar(table_sb[:, 0:P], bank_y[0:H, 0:P], b2_col[:, :], None, ALU.add).then_inc(net_step, 1)

            def x_stats(m):
                wait(e, x_loaded, m, by=16)
                e.bn_stats(moments[:, 0, :], x_in[:, :]).then_inc(x_moments, 1)

            def y_stats(m):
                wait(e, wo_half[1], m)
                e.bn_stats(moments[:, 1, :], bank_y[:, :]).then_inc(y_moments, 1)

            def means_variances(at):
                last = None
                for i, (d, stats) in enumerate(((3, x_moments), (-1, y_moments))):
                    if at(d) is not None:
                        wait(e, stats, at(d))
                        e.nop(nofuse=True)
                        last = e.bn_aggr(mean_var[:, i, :], moments[:, i, :])
                last.then_inc(mean_var_done, 1)
                e.wait_ge(mean_var_done, step_count(at))
                e.tensor_scalar(var_eps[:, :], mean_var[:, :, 1], EPS, None, ALU.add).then_inc(var_eps_done, 1)

            def ln_apply(m):
                wait(e, rstd_done, m)
                wait(e, xt_psum, m, -1)
                e.tensor_scalar(xn[:, :], x_in[:, :], mean_var[:, 0, 0:1], rstd[:, 0:1], ALU.subtract, ALU.mult)\
                    .then_inc(xn_ready, 1)

            def split_xt(m):
                wait(e, xt_h_ready, m)
                e.tensor_tensor(xt_l[:, :, :], bank_t[:, :].rearrange("p (c t) -> p c t", c=KC),
                                xt_h[:, :, :].bitcast(F32), ALU.subtract).then_inc(xt_ready, 1)

            def q_sums(m, p):
                if m[0] == 0:
                    return
                first, n = PARTS[p]
                n += p == 2
                wait_in_layer1(e, squares_ready[p], m)
                e.reduce_sum(ss[:, first:first + n], squares[:, 0:n * DH].rearrange("p (h d) -> p h d", h=n), AX.X)\
                    .then_inc(q_sum[p], 1)

            def q_scale_out(m, p):
                first, n = PARTS[p]
                bank = bank_q[p % 2]
                if m[0] == 1:
                    wait_in_layer1(e, q_norm[p], m)
                    wait(e, qt_psum[1], m, -1)
                    last = e.tensor_tensor(
                        q_nat[:, first * DH:(first + n) * DH].rearrange("p (h d) -> p h d", h=n),
                        bank[:, 0:n * DH].rearrange("p (h d) -> p h d", h=n),
                        rnorm[:, first:first + n].unsqueeze(2).broadcast_to([P, n, DH]), ALU.mult)
                    if p < 2:
                        last.then_inc(q_done[p], 1)
                if p < 2:
                    return
                k0, v0, s0 = n * DH, (n + 1) * DH, (n + 2) * DH
                k2 = bank[:, k0:v0].unsqueeze(1).broadcast_to([P, 2, DH])
                wait(e, kt_psum, m, -1)
                if m[0] == 0:
                    wait(e, q_copied, m)
                    e.tensor_scalar(k_nat[:, :, :], k2, DH ** -0.5, None, ALU.mult)
                    e.scalar_tensor_tensor(out=nns_next[:, :], in0=bank[:, s0:s0 + H], scalar=-1.0,
                                           in1=null_bias_sb[:, 0, :], op0=ALU.mult, op1=ALU.subtract)\
                        .then_inc(nns_next_ready, 1)
                else:
                    e.scalar_tensor_tensor(out=k_nat[:, :, :], in0=k2, scalar=rnorm[:, H:H + 1],
                                           in1=k_mul[:, :].unsqueeze(1).broadcast_to([P, 2, DH]),
                                           op0=ALU.mult, op1=ALU.mult)
                    e.tensor_tensor(null_s[:, :], bank[:, s0:s0 + H], rnorm[:, 0:H], ALU.mult)\
                        .then_inc(null_s_done, 1)
                    wait_in_layer1(e, null_s_done, m)
                    e.scalar_tensor_tensor(out=nns_next[:, :], in0=null_s[:, :], scalar=-1.0,
                                           in1=null_bias_sb[:, 1, :], op0=ALU.mult, op1=ALU.subtract)\
                        .then_inc(nns_next_ready, 1)
                wait(e, v_ready, m, -1)
                e.tensor_tensor(v_raw[:, :], bank[:, v0:s0], null_v[:, :], ALU.subtract).then_inc(q_done[2], 1)

            def split_qt(m, half):
                wait(e, qt_h_ready[half], m)
                e.tensor_tensor(qt_l[:, 4 * half:4 * half + 4, :], bank_t[:, :].rearrange("p (c t) -> p c t", c=4),
                                qt_h[:, 4 * half:4 * half + 4, :].bitcast(F32), ALU.subtract)\
                    .then_inc(qt_ready[half], 1)

            def split_kt(m):
                wait(e, kt_h_ready, m)
                for half in range(2):
                    r = slice(half * DH, (half + 1) * DH)
                    last = e.tensor_tensor(kt_l[r, half, :], bank_t[r, 0:P], kt_h[r, half, :].bitcast(F32), ALU.subtract)
                last.then_inc(kt_ready, 1)

            def split_v(m):
                wait(e, v_h_ready, m)
                h2 = v_h[:, :].rearrange("p (a b d) -> p a b d", a=2, b=2)
                l2 = v_l[:, :].rearrange("p (a b d) -> p a b d", a=2, b=2)
                for half in range(2):
                    last = e.tensor_tensor(l2[:, half, half, :], v_raw[:, :], h2[:, half, half, :].bitcast(F32),
                                           ALU.subtract)
                last.then_inc(v_ready, 1)

            def take_null_scores(m):
                wait(e, nns_next_ready, m)
                e.tensor_copy(nns[:, :], nns_next[:, :]).then_inc(nns_ready, 1)

            def take_mask(m):
                if opens_layer(m):
                    e.wait_ge(rows_loaded, 16 * ROW_LOADS)
                wait(e, bias_ready[3], m, -1)
                e.tensor_scalar(mask_row[:, :], mask[:, m[0], m[1], :], -1.0, BIG, ALU.add, ALU.mult)\
                    .then_inc(mask_ready, 1)

            def scores(m, g):
                hs = slice(HG * g, HG * (g + 1))
                wait(e, s_psum[g], m)
                wait(e, bias_ready[g], m)
                wait(e, exp_ready[(g + 2) % G], m, -1 if g < 2 else 0)
                if g == 0:
                    wait(e, nns_ready, m)
                e.tensor_scalar(s_sb[:, g % 2, :, P], nns[:, hs], -1.0, None, ALU.mult)
                for j in range(HG):
                    h = HG * g + j
                    last = e.tensor_tensor_reduce(s_sb[:, g % 2, j, 0:P], bank_s[g % 2][:, j * P:(j + 1) * P],
                                                  bias_g[:, g % 2, j, :], 1.0, LOWEST, ALU.add, ALU.max,
                                                  mx[:, h:h + 1])
                last.then_inc(s_ready[g], 1)
                wait(e, s_ready[g], m)
                e.scalar_tensor_tensor(out=neg_m[:, hs], in0=mx[:, hs], scalar=-1.0, in1=nns[:, hs],
                                       op0=ALU.mult, op1=ALU.min).then_inc(neg_m_ready[g], 1)

            def sums(m, g):
                hs = slice(HG * g, HG * (g + 1))
                wait(e, exp_ready[g], m)
                e.reciprocal(rden[:, hs], esum[:, hs]).then_inc(rden_ready[g], 1)

            def split_pt(m, g):
                wait(e, pt_h_ready[g], m)
                e.tensor_tensor(pt_l[:, g % 2, :, :], bank_p[:, :].rearrange("p (h i) -> p h i", h=HG),
                                pt_h[:, g % 2, :, :].bitcast(F32), ALU.subtract).then_inc(pt_ready[g], 1)

            def split_ot(m, half):
                cs = slice(4 * half, 4 * half + 4)
                wait(e, ot_h_ready[half], m)
                e.scalar_tensor_tensor(out=ot_l[:, cs, :], in0=bank_o[:, :].rearrange("p (c t) -> p c t", c=4),
                                       scalar=null_v_col[:, :], in1=ot_h[:, cs, :].bitcast(F32),
                                       op0=ALU.add, op1=ALU.subtract).then_inc(ot_ready[half], 1)

            def y_center(m):
                wait(e, mean_var_done, m, 4)
                e.scalar_tensor_tensor(out=y_t, in0=bank_y[:, :], scalar=mean_var[:, 1, 0:1], in1=g_out_sb[:, m[0], :],
                                       op0=ALU.subtract, op1=ALU.mult).then_inc(y_out_of_psum, 1)

            def y_finish(m):
                wait(e, rstd_done, m, 4)
                wait(e, y_out_of_psum, m)
                wait(e, res_loaded, m, by=16)
                wait(e, x_stored, m, -1, by=16)
                e.scalar_tensor_tensor(out=x_out, in0=y_t, scalar=rstd[:, 1:2], in1=x_res[:, :],
                                       op0=ALU.mult, op1=ALU.add).then_inc(x_out_ready, 1)

            def step(at):
                def on(d, stage, *which):
                    if at(d) is not None:
                        stage(at(d), *which)

                on(1, split_xt)
                on(1, start_sums)
                on(0, scores, 0)
                on(2, ln_apply)
                on(2, start_first_part)
                on(1, start_weights)
                on(0, scores, 1)
                on(0, sums, 0)
                on(1, q_sums, 0)
                on(0, scores, 2)
                on(0, sums, 1)
                on(1, q_scale_out, 0)
                on(1, next_weights, 0)
                on(1, q_sums, 1)
                on(0, scores, 3)
                on(1, q_scale_out, 1)
                on(1, next_weights, 1)
                on(0, split_v)
                on(1, q_sums, 2)
                on(0, split_pt, 0)
                on(0, sums, 2)
                on(-1, split_ot, 1)
                on(0, start_table)
                on(1, split_qt, 0)
                on(1, start_silu, [0])
                on(1, q_scale_out, 2)
                on(1, next_weights, 2)
                on(0, split_pt, 1)
                on(-1, next_output, 0)
                on(0, sums, 3)
                on(1, take_null_scores)
                on(1, take_mask)
                on(3, x_stats)
                on(1, split_qt, 1)
                on(1, start_silu, [1])
                on(0, split_pt, 2)
                on(-1, y_stats)
                on(1, split_kt)
                on(1, start_silu, [2, 3])
                means_variances(at)
                on(0, split_ot, 0)
                on(-1, y_center)
                on(0, split_pt, 3)
                on(-1, next_output, 1)
                on(-1, y_finish)

            def start_sums(m):
                if is_item(m, 0, 0):
                    for c in range(KC - 1):
                        null_sum(0, c)

            def start_first_part(m):
                if is_item(m, 0, 0):
                    project_weights(0, 0)

            def start_weights(m):
                if is_item(m, 0, 0):
                    project_weights(0, 2)
                    net_second_layer()

            def start_silu(m, quarters):
                if is_item(m, 0, 0):
                    net_silu(EXP2, PLUS2, REC2, quarters)

            def start_table(m):
                if is_item(m, 0, 0):
                    net_table()

            def next_output(m, half):
                if is_item(m, 0, B - 1):
                    output_weights(1, half)

            def next_weights(m, p):
                if is_item(m, 0, B - 1):
                    project_weights(1, p)

            def between(n):
                if n == -1:
                    project_weights(0, 1)
                if n in NULL_STEPS:
                    null_sum(1, NULL_STEPS.index(n))

            net_first_layer()
            stream(e, step, between)

        @block.tensor
        def _(e):
            e.wait_ge(consts_ready, 4)

            def product(out, passes):
                for k, (a, b) in enumerate(passes):
                    last = e.matmul(out, a, b, start=(k == 0), stop=(k == len(passes) - 1))
                return last

            def net_transposes(silu, tp):
                e.wait_ge(net_step, silu)
                for c in range(KC):
                    last = e.transpose(bank_t[:, c * P:(c + 1) * P], net[:, c * P:(c + 1) * P], ident[:, :])
                last.then_inc(net_step, 1)

            net_transposes(SILU1, TP1)

            def start_product(m):
                if is_item(m, 0, 0):
                    e.wait_ge(net_step, TCOPY1)
                    product(bank_y[:, :], [(net_t[:, c, :], w1_sb[:, c, :]) for c in range(KC)]).then_inc(net_step, 1)

            def start_table(m):
                if is_item(m, 0, 0):
                    wait(e, xt_ready, m, 1)
                    net_transposes(SILU2, TP2)
                    e.wait_ge(net_step, TCOPY2)
                    product(bank_y[0:H, 0:P], [(w2_sb[:, c, :], net_t[:, c, :]) for c in range(KC)])\
                        .then_inc(net_step, 1)

            def transpose_x(m):
                wait(e, xn_ready, m)
                if opens_layer(m) and m[0] == 0:
                    e.wait_ge(net_step, TCOPY1)
                else:
                    wait(e, kt_ready, m, -1)
                for c in range(KC):
                    last = e.transpose(bank_t[:, c * P:(c + 1) * P], xn[:, c * P:(c + 1) * P], ident[:, :])
                last.then_inc(xt_psum, 1)

            def project(m, p):
                lo, hi = part_columns(p)
                if opens_layer(m):
                    e.wait_ge(wq_ready[p], m[0] + 1)
                if p == 0:
                    wait(e, xt_ready, m)
                    wait(e, q_done[2], m, -1)
                elif p == 1:
                    wait(e, q_done[1], m, -1)
                else:
                    wait(e, q_done[0], m)
                passes = []
                for c in range(KC):
                    passes += [(xt_h[:, c, :], wq_h[:, c, lo:hi]), (xt_h[:, c, :], wq_l[:, c, lo:hi]),
                               (xt_l[:, c, :], wq_h[:, c, lo:hi])]
                product(bank_q[p % 2][:, 0:hi - lo], passes).then_inc(q_psum[p], 1)

            def transpose_q(m, half):
                if half == 0:
                    wait(e, q_done[0], m)
                    wait(e, q_done[1], m)
                    wait(e, xt_ready, m)
                else:
                    wait(e, q_done[2], m)
                    wait(e, qt_ready[0], m)
                for c in range(4):
                    k = 4 * half + c
                    last = e.transpose(bank_t[:, c * P:(c + 1) * P], q_nat[:, k * P:(k + 1) * P], ident[:, :])
                last.then_inc(qt_psum[half], 1)

            def transpose_k(m):
                wait(e, qt_ready[1], m)
                e.transpose(bank_t[:, 0:P], k_nat[:, :, :].rearrange("p a d -> p (a d)"), ident[:, :])\
                    .then_inc(kt_psum, 1)

            def scores(m, g):
                if g % 2 == 0:
                    wait(e, qt_ready[g // 2], m)
                if g == 0:
                    wait(e, kt_ready, m)
                wait(e, s_ready[(g + 2) % G], m, -1 if g < 2 else 0)
                kh, kl = (t[:, :, :].rearrange("p a j -> p (a j)") for t in (kt_h, kt_l))
                for j in range(2):
                    c = 2 * g + j
                    last = product(bank_s[g % 2][:, j * 2 * P:(j + 1) * 2 * P],
                                   [(qt_h[:, c, :], kh), (qt_h[:, c, :], kl), (qt_l[:, c, :], kh)])
                last.then_inc(s_psum[g], 1)

            def transpose_p(m, g):
                wait(e, p_ready[g], m)
                wait(e, pt_ready[(g + 3) % G], m, -1 if g == 0 else 0)
                for j in range(HG):
                    last = e.transpose(bank_p[:, j * P:(j + 1) * P], p_sb[:, g % 2, j, :], ident[:, :])
                last.then_inc(pt_psum[g], 1)

            def attend(m, g):
                wait(e, pt_ready[g], m)
                if g == 0:
                    wait(e, v_ready, m)
                if g % 2 == 0:
                    wait(e, ot_ready[1 - g // 2], m, -1 if g == 0 else 0)
                passes = []
                for odd in range(2):
                    vh, vl = (t[:, odd * P:(odd + 1) * P] for t in (v_h, v_l))
                    ph, pl = (t[:, g % 2, odd::2, :] for t in (pt_h, pt_l))
                    passes += [(vh, ph), (vl, ph), (vh, pl)]
                o = bank_o[:, (g % 2) * 2 * P:(g % 2 + 1) * 2 * P].rearrange("p (c i) -> p c i", c=2)
                product(o, passes).then_inc(pv_psum[g], 1)

            def output(m, c0, c1):
                if opens_layer(m) and c0 % 4 == 0:
                    e.wait_ge(wo_ready, 2 * m[0] + c0 // 4 + 1)
                if is_item(m, 0, 0) and c0 == 0:
                    e.wait_ge(net_step, TABLE)
                if c0 == 0:
                    wait(e, y_out_of_psum, m, -1)
                if c0 % 4 == 0:
                    wait(e, ot_ready[c0 // 4], m)
                for c in range(c0, c1):
                    for k, (a, b) in enumerate(((ot_h, wo_h), (ot_h, wo_l), (ot_l, wo_h))):
                        last = e.matmul(bank_y[:, :], a[:, c, :], b[:, c, :], start=(c == 0 and k == 0),
                                        stop=(c == OC - 1 and k == 2))
                if c1 % 4 == 0:
                    last.then_inc(wo_half[c1 // 4 - 1], 1)

            def step(at):
                def on(d, stage, *which):
                    if at(d) is not None:
                        stage(at(d), *which)

                on(0, scores, 0)
                on(1, transpose_x)
                on(1, start_product)
                on(-1, attend, 2)
                on(0, scores, 1)
                on(-1, output, 0, 2)
                on(1, project, 0)
                on(0, scores, 2)
                on(1, project, 1)
                on(0, transpose_p, 0)
                on(0, scores, 3)
                on(-1, attend, 3)
                on(1, project, 2)
                on(0, start_table)
                on(1, transpose_q, 0)
                on(-1, output, 2, 4)
                on(0, transpose_p, 1)
                on(-1, output, 4, 6)
                on(0, attend, 0)
                on(1, transpose_q, 1)
                on(0, transpose_p, 2)
                on(-1, output, 6, 8)
                on(1, transpose_k)
                on(0, attend, 1)
                on(0, transpose_p, 3)

            stream(e, step)


_INS = ["x", "fside_16xSxS_0", "cond_64", "mask_BxS_bk0", "mask_BxS_bf1",
        "L0_cond_g_in", "L0_cond_null_attn_bias", "L0_cond_Wq", "L0_cond_Wkv", "L0_cond_Wo", "L0_cond_g_out",
        "L1_cond_g_norm", "L1_cond_Wq", "L1_cond_Wkv", "L1_cond_q_scale", "L1_cond_k_scale",
        "L1_cond_null_attn_bias", "L1_cond_w0", "L1_cond_b0", "L1_cond_g0", "L1_cond_w1", "L1_cond_b1",
        "L1_cond_g1", "L1_cond_w2", "L1_cond_b2", "L1_cond_Wout", "L1_cond_g_out"]


def kernel(**inputs):
    import numpy as _np
    import concourse.bacc as _bacc
    from concourse import mybir as _mybir
    from concourse.bass_utils import run_bass_kernel_spmd as _run

    nc = _bacc.Bacc("TRN2", target_bir_lowering=False, num_devices=1)
    arrays, a = {}, {}
    for name in _INS:
        v = _np.ascontiguousarray(inputs[name])
        arrays[f"in_{name}"] = v
        a[name] = nc.dram_tensor(f"in_{name}", v.shape, _mybir.dt.from_np(v.dtype), kind="ExternalInput").ap()
    out = nc.dram_tensor("out_x", (B, P, D), F32, kind="ExternalOutput").ap()
    build(nc, a["x"], a["fside_16xSxS_0"], a["cond_64"], a["mask_BxS_bk0"], a["mask_BxS_bf1"],
          [a["L0_cond_g_in"], a["L1_cond_g_norm"]],
          [a["L0_cond_null_attn_bias"], a["L1_cond_null_attn_bias"]],
          [a["L0_cond_Wq"], a["L1_cond_Wq"]], [a["L0_cond_Wkv"], a["L1_cond_Wkv"]],
          [a["L0_cond_Wo"], a["L1_cond_Wout"]], [a["L0_cond_g_out"], a["L1_cond_g_out"]],
          a["L1_cond_q_scale"], a["L1_cond_k_scale"], a["L1_cond_w0"], a["L1_cond_b0"], a["L1_cond_g0"],
          a["L1_cond_w1"], a["L1_cond_b1"], a["L1_cond_g1"], a["L1_cond_w2"], a["L1_cond_b2"], out)
    r = _run(nc, [arrays], core_ids=[0])
    return r.results[0]["out_x"]
```
